# Optimizing a Trainium2 kernel written in Bass

```python
import numpy as np
import jax
import jax.numpy as jnp

def _softmax(x, axis=-1):
    return jax.nn.softmax(x, axis=axis)

def _gelu(x):
    return jax.nn.gelu(x, approximate=True)

def _silu(x):
    return jax.nn.silu(x)

def _sigmoid(x):
    return jax.nn.sigmoid(x)

def _layernorm(x, axis=-1, eps=1e-05):
    m = jnp.mean(x, axis=axis, keepdims=True)
    v = jnp.var(x, axis=axis, keepdims=True)
    return (x - m) / jnp.sqrt(v + eps)

def _scatter_add(tgt, idx, src, axis=0):
    return tgt.at[idx].add(src)

def _segment_sum(src, seg, n):
    return jax.ops.segment_sum(src, seg, n)
kernel_name = 'mk_vit_tower_postln_d2_tok_img768_r4_b79022'

def setup_inputs(seed: int=0):
    np.random.seed(seed)
    _w = jnp.asarray

    def _rec_inputs():
        import jax
        import jax.numpy as jnp
        _rk = jax.random.key(seed)
        x = -0.000356955 + 1 * jax.random.normal(jax.random.fold_in(_rk, 1), (32, 3, 96, 96), jnp.float32)
        return x
    x = _rec_inputs()

    def _L0_tok_setup():
        import jax, jax.numpy as jnp
        import numpy as np
        PATCH = 16
        POS_GRID = (14, 14)
        EMBED = 192
        C_IN = 3

        def _nearest_resize(x, out_h, out_w):
            _, _, h, w = x.shape
            ih = jnp.arange(out_h) * h // out_h
            iw = jnp.arange(out_w) * w // out_w
            return x[:, :, ih][:, :, :, iw]
        key = jax.random.key(seed)
        k1, k2, k3, k4, k5 = jax.random.split(key, 5)
        im = jax.random.normal(k1, (128, C_IN, 224, 224), dtype=jnp.float32)
        W = jax.random.normal(k2, (C_IN * PATCH * PATCH, EMBED), dtype=jnp.float32) * 0.02
        b = jax.random.normal(k3, (EMBED,), dtype=jnp.float32) * 0.02
        positions = jax.random.normal(k4, (1, EMBED, POS_GRID[0], POS_GRID[1]), dtype=jnp.float32)
        cls_embedding = jax.random.normal(k5, (1, 1, EMBED), dtype=jnp.float32)
        return {'im': im, 'W': W, 'b': b, 'positions': positions, 'cls_embedding': cls_embedding}
    _L0_tok_all = _L0_tok_setup()
    _L0_tok_in = {k: v for k, v in _L0_tok_all.items() if k in ('W', 'b', 'positions', 'cls_embedding')}
    del _L0_tok_all

    def _L0_attn_setup():
        import jax, jax.numpy as jnp
        import numpy as np
        from jax import lax
        NUM_HEADS = 12
        BETA = 0.2
        KS = 3
        LN_EPS = 1e-05
        key = jax.random.key(seed)
        k1, k2 = jax.random.split(key)
        B, N, C = (4, 256, 192)
        x = jax.random.normal(k1, (B, N, C), dtype=jnp.float32)
        qkv_w = jax.random.normal(k2, (3 * C, C), dtype=jnp.float32) * 0.02
        qkv_b = jnp.zeros((3 * C,), dtype=jnp.float32)
        ln_g = jnp.ones((C,), dtype=jnp.float32)
        ln_b = jnp.zeros((C,), dtype=jnp.float32)
        return {'x': x, 'qkv_w': qkv_w, 'qkv_b': qkv_b, 'ln_g': ln_g, 'ln_b': ln_b}
    _L0_attn_all = _L0_attn_setup()
    _L0_attn_in = {k: v for k, v in _L0_attn_all.items() if k in ('qkv_w', 'qkv_b', 'ln_g', 'ln_b')}
    del _L0_attn_all

    def _L0_ffn_setup():
        import jax, jax.numpy as jnp
        import numpy as np
        import math
        N_HEAD = 12
        N_EXP = 8
        TOP_K = 2
        EVAL_CAPACITY = 1.0
        MIN_CAPACITY = 4
        EPS = 1e-05

        def layer_norm(x, w):
            mu = jnp.mean(x, axis=-1, keepdims=True)
            var = jnp.var(x, axis=-1, keepdims=True)
            return (x - mu) / jnp.sqrt(var + EPS) * w

        def attention(x, c_attn_w, c_proj_w):
            B, T, C = x.shape
            H, D = (N_HEAD, C // N_HEAD)
            qkv = x @ c_attn_w.T
            q, k, v = jnp.split(qkv, 3, axis=-1)
            q = q.reshape(B, T, H, D).transpose(0, 2, 1, 3)
            k = k.reshape(B, T, H, D).transpose(0, 2, 1, 3)
            v = v.reshape(B, T, H, D).transpose(0, 2, 1, 3)
            scores = jnp.einsum('bhqd,bhkd->bhqk', q, k) * (1.0 / math.sqrt(D))
            causal = jnp.tril(jnp.ones((T, T), dtype=bool))
            scores = jnp.where(causal, scores, -jnp.inf)
            att = jax.nn.softmax(scores, axis=-1)
            y = jnp.einsum('bhqk,bhkd->bhqd', att, v)
            y = y.transpose(0, 2, 1, 3).reshape(B, T, C)
            return y @ c_proj_w.T

        def get_capacity(num_tokens):
            cap = int(math.floor(TOP_K * EVAL_CAPACITY * num_tokens / N_EXP))
            cap += cap % 2
            return max(cap, MIN_CAPACITY)

        def moe(x_flat, w_g, c_fc, c_proj_e):
            n_tok, C = x_flat.shape
            logits = x_flat @ w_g.T
            top_vals, top_idx = jax.lax.top_k(logits, TOP_K)
            rows = jnp.arange(n_tok)[:, None]
            masked = jnp.full_like(logits, -jnp.inf).at[rows, top_idx].set(top_vals)
            probs = jax.nn.softmax(masked, axis=-1)
            cap = get_capacity(n_tok)
            flat_e = top_idx.reshape(-1)
            onehot = jax.nn.one_hot(flat_e, N_EXP, dtype=jnp.int32)
            pos = jnp.cumsum(onehot, axis=0) - onehot
            slot = jnp.take_along_axis(pos, flat_e[:, None], axis=1)[:, 0]
            valid = slot < cap
            tok = jnp.repeat(jnp.arange(n_tok), TOP_K)
            slot_c = jnp.where(valid, slot, cap)
            sec = jnp.zeros((n_tok, N_EXP, cap + 1), dtype=x_flat.dtype)
            sec = sec.at[tok, flat_e, slot_c].set(1.0)[:, :, :cap]
            w_tok = probs[tok, flat_e]
            cb = jnp.zeros((n_tok, N_EXP, cap + 1), dtype=x_flat.dtype)
            cb = cb.at[tok, flat_e, slot_c].set(w_tok)[:, :, :cap]
            dispatched = jnp.einsum('tec,td->ecd', sec, x_flat)
            h = jax.nn.gelu(jnp.einsum('ecd,edh->ech', dispatched, c_fc), approximate=False)
            out = jnp.einsum('ech,ehd->ecd', h, c_proj_e)
            return jnp.einsum('tec,ecd->td', cb, out)
        key = jax.random.key(seed)
        ks = jax.random.split(key, 7)
        B, T, C = (2, 512, 192)
        std = 0.02
        return {'x': jax.random.normal(ks[0], (B, T, C), dtype=jnp.float32), 'ln1_w': jnp.ones((C,), dtype=jnp.float32), 'ln2_w': jnp.ones((C,), dtype=jnp.float32), 'c_attn_w': jax.random.normal(ks[1], (3 * C, C), dtype=jnp.float32) * std, 'c_proj_w': jax.random.normal(ks[2], (C, C), dtype=jnp.float32) * std, 'w_g': jax.random.normal(ks[3], (N_EXP, C), dtype=jnp.float32) * std, 'c_fc': jax.random.normal(ks[4], (N_EXP, C, 4 * C), dtype=jnp.float32) * std, 'c_proj_e': jax.random.normal(ks[5], (N_EXP, 4 * C, C), dtype=jnp.float32) * std}
    _L0_ffn_all = _L0_ffn_setup()
    _L0_ffn_in = {k: v for k, v in _L0_ffn_all.items() if k in ('ln1_w', 'ln2_w', 'c_attn_w', 'c_proj_w', 'w_g', 'c_fc', 'c_proj_e')}
    del _L0_ffn_all

    def _L1_attn_setup():
        import jax, jax.numpy as jnp
        import numpy as np
        B, N, DIM = (64, 197, 192)
        H = 12
        IN_DIM = 192
        HD = IN_DIM // H
        key = jax.random.key(seed)
        k1, k2, k3 = jax.random.split(key, 3)
        x = jax.random.normal(k1, (B, N, DIM), dtype=jnp.float32)
        scale = (DIM // H) ** (-0.5) * jnp.ones((H,), dtype=jnp.float32)
        w_qkv = jax.random.normal(k2, (3 * IN_DIM, DIM), dtype=jnp.float32) * 0.02
        w_proj = jax.random.normal(k3, (IN_DIM, IN_DIM), dtype=jnp.float32) * 0.02
        b_proj = jnp.zeros((IN_DIM,), dtype=jnp.float32)
        return {'x': x, 'scale': scale, 'w_qkv': w_qkv, 'w_proj': w_proj, 'b_proj': b_proj}
    _L1_attn_all = _L1_attn_setup()
    _L1_attn_in = {k: v for k, v in _L1_attn_all.items() if k in ('scale', 'w_qkv', 'w_proj', 'b_proj')}
    del _L1_attn_all

    def _L1_ffn_setup():
        import jax, jax.numpy as jnp
        import numpy as np
        B, S, D, F = (2, 128, 192, 768)
        L, H, DK = (4, 12, 64)
        E, K = (8, 2)
        NB, MAXD = (32, 128)
        MOE_LAYERS = (1, 3)
        EPS = 1e-06

        def t5_layer_norm(x, w):
            var = jnp.mean(x * x, axis=-1, keepdims=True)
            return w * x * jax.lax.rsqrt(var + EPS)

        def relative_position_bias(rel_emb, seq_len):
            ctx = jnp.arange(seq_len)[:, None]
            mem = jnp.arange(seq_len)[None, :]
            rel = mem - ctx
            nb = NB // 2
            buckets = (rel > 0).astype(jnp.int32) * nb
            n = jnp.abs(rel)
            max_exact = nb // 2
            is_small = n < max_exact
            nf = jnp.maximum(n, 1).astype(jnp.float32)
            large = max_exact + (jnp.log(nf / max_exact) / np.log(MAXD / max_exact) * (nb - max_exact)).astype(jnp.int32)
            large = jnp.minimum(large, nb - 1)
            buckets = buckets + jnp.where(is_small, n, large)
            return rel_emb[buckets].transpose(2, 0, 1)[None]

        def moe_ffn(x2d, gw, w1, w2):
            logits = x2d @ gw
            vals, idx = jax.lax.top_k(logits, K)
            gsc = jax.nn.softmax(vals, axis=-1)
            T = x2d.shape[0]
            cw = jnp.zeros((T, E), x2d.dtype).at[jnp.arange(T)[:, None], idx].add(gsc)

            def body(acc, xs):
                w1e, w2e, cwe = xs
                y = jax.nn.gelu(x2d @ w1e, approximate=False) @ w2e
                return (acc + cwe[:, None] * y, None)
            out, _ = jax.lax.scan(body, jnp.zeros_like(x2d), (w1, w2, cw.T))
            return out
        key = jax.random.key(seed)
        ks = list(jax.random.split(key, 16))

        def nrm(k, shape, scale=0.02):
            return jax.random.normal(k, shape, jnp.float32) * scale
        M = len(MOE_LAYERS)
        return {'x': nrm(ks[0], (B, S, D), 1.0), 'attn_q': nrm(ks[1], (L, D, H * DK)), 'attn_k': nrm(ks[2], (L, D, H * DK)), 'attn_v': nrm(ks[3], (L, D, H * DK)), 'attn_o': nrm(ks[4], (L, H * DK, D)), 'ffn_wi': nrm(ks[5], (L, D, F)), 'ffn_wo': nrm(ks[6], (L, F, D)), 'ln1': jnp.ones((L, D), jnp.float32), 'ln2': jnp.ones((L, D), jnp.float32), 'ln_f': jnp.ones((D,), jnp.float32), 'rel_emb': nrm(ks[7], (NB, H), 0.1), 'gate_w': nrm(ks[8], (M, D, E)), 'moe_w1': nrm(ks[9], (M, E, D, F)), 'moe_w2': nrm(ks[10], (M, E, F, D))}
    _L1_ffn_all = _L1_ffn_setup()
    _L1_ffn_in = {k: v for k, v in _L1_ffn_all.items() if k in ('attn_q', 'attn_k', 'attn_v', 'attn_o', 'ffn_wi', 'ffn_wo', 'ln1', 'ln2', 'ln_f', 'rel_emb', 'gate_w', 'moe_w1', 'moe_w2')}
    del _L1_ffn_all
    return {'x': x, 'L0_tok_W': _L0_tok_in['W'], 'L0_tok_b': _L0_tok_in['b'], 'L0_tok_positions': _L0_tok_in['positions'], 'L0_tok_cls_embedding': _L0_tok_in['cls_embedding'], 'L0_attn_qkv_w': _L0_attn_in['qkv_w'], 'L0_attn_qkv_b': _L0_attn_in['qkv_b'], 'L0_attn_ln_g': _L0_attn_in['ln_g'], 'L0_attn_ln_b': _L0_attn_in['ln_b'], 'L0_ffn_ln1_w': _L0_ffn_in['ln1_w'], 'L0_ffn_ln2_w': _L0_ffn_in['ln2_w'], 'L0_ffn_c_attn_w': _L0_ffn_in['c_attn_w'], 'L0_ffn_c_proj_w': _L0_ffn_in['c_proj_w'], 'L0_ffn_w_g': _L0_ffn_in['w_g'], 'L0_ffn_c_fc': _L0_ffn_in['c_fc'], 'L0_ffn_c_proj_e': _L0_ffn_in['c_proj_e'], 'L1_attn_scale': _L1_attn_in['scale'], 'L1_attn_w_qkv': _L1_attn_in['w_qkv'], 'L1_attn_w_proj': _L1_attn_in['w_proj'], 'L1_attn_b_proj': _L1_attn_in['b_proj'], 'L1_ffn_attn_q': _L1_ffn_in['attn_q'], 'L1_ffn_attn_k': _L1_ffn_in['attn_k'], 'L1_ffn_attn_v': _L1_ffn_in['attn_v'], 'L1_ffn_attn_o': _L1_ffn_in['attn_o'], 'L1_ffn_ffn_wi': _L1_ffn_in['ffn_wi'], 'L1_ffn_ffn_wo': _L1_ffn_in['ffn_wo'], 'L1_ffn_ln1': _L1_ffn_in['ln1'], 'L1_ffn_ln2': _L1_ffn_in['ln2'], 'L1_ffn_ln_f': _L1_ffn_in['ln_f'], 'L1_ffn_rel_emb': _L1_ffn_in['rel_emb'], 'L1_ffn_gate_w': _L1_ffn_in['gate_w'], 'L1_ffn_moe_w1': _L1_ffn_in['moe_w1'], 'L1_ffn_moe_w2': _L1_ffn_in['moe_w2']}

def reference(x, L0_tok_W, L0_tok_b, L0_tok_positions, L0_tok_cls_embedding, L0_attn_qkv_w, L0_attn_qkv_b, L0_attn_ln_g, L0_attn_ln_b, L0_ffn_ln1_w, L0_ffn_ln2_w, L0_ffn_c_attn_w, L0_ffn_c_proj_w, L0_ffn_w_g, L0_ffn_c_fc, L0_ffn_c_proj_e, L1_attn_scale, L1_attn_w_qkv, L1_attn_w_proj, L1_attn_b_proj, L1_ffn_attn_q, L1_ffn_attn_k, L1_ffn_attn_v, L1_ffn_attn_o, L1_ffn_ffn_wi, L1_ffn_ffn_wo, L1_ffn_ln1, L1_ffn_ln2, L1_ffn_ln_f, L1_ffn_rel_emb, L1_ffn_gate_w, L1_ffn_moe_w1, L1_ffn_moe_w2):
    import jax
    import jax.numpy as jnp

    def _L0_tok_ref(im, W, b, positions, cls_embedding):
        import jax, jax.numpy as jnp
        import numpy as np
        PATCH = 16
        POS_GRID = (14, 14)
        EMBED = 192
        C_IN = 3

        def _nearest_resize(x, out_h, out_w):
            _, _, h, w = x.shape
            ih = jnp.arange(out_h) * h // out_h
            iw = jnp.arange(out_w) * w // out_w
            return x[:, :, ih][:, :, :, iw]
        B, C, H, Wd = im.shape
        ph, pw = (PATCH, PATCH)
        gh, gw = (H // ph, Wd // pw)
        patches = im.reshape(B, C, gh, ph, gw, pw)
        patches = patches.transpose(0, 2, 4, 1, 3, 5).reshape(B, gh * gw, C * ph * pw)
        pos = _nearest_resize(positions, gh, gw)
        pos = pos.reshape(1, EMBED, gh * gw).transpose(0, 2, 1)
        embeds = jnp.einsum('bsp,pd->bsd', patches, W) + b + pos
        cls_tok = jnp.broadcast_to(cls_embedding, (B, 1, EMBED))
        return jnp.concatenate((cls_tok, embeds), axis=1)

    def _L0_attn_ref(x, qkv_w, qkv_b, ln_g, ln_b):
        import jax, jax.numpy as jnp
        import numpy as np
        from jax import lax
        NUM_HEADS = 12
        BETA = 0.2
        KS = 3
        LN_EPS = 1e-05
        B, N, C = x.shape
        H = NUM_HEADS
        D = C // H
        mu = jnp.mean(x, axis=-1, keepdims=True)
        var = jnp.mean(jnp.square(x - mu), axis=-1, keepdims=True)
        xn = (x - mu) * lax.rsqrt(var + LN_EPS) * ln_g + ln_b
        qkv = xn @ qkv_w.T + qkv_b
        qkv = qkv.reshape(B, N, 3, H, D).transpose(2, 0, 3, 1, 4)
        q, k, v = (qkv[0], qkv[1], qkv[2])
        attn = jnp.einsum('bhnd,bhmd->bhnm', q, k) * D ** (-0.5)
        kernel = jnp.ones((KS, KS), dtype=attn.dtype).at[KS // 2, KS // 2].set(0.0)
        kernel = kernel.reshape(1, 1, KS, KS)
        neigh = lax.conv_general_dilated(attn.reshape(B * H, 1, N, N), kernel, window_strides=(1, 1), padding='SAME', dimension_numbers=('NCHW', 'OIHW', 'NCHW'))
        attn = attn - BETA * neigh.reshape(B, H, N, N)
        attn = jax.nn.softmax(attn - jnp.max(attn, axis=-1, keepdims=True), axis=-1)
        out = jnp.einsum('bhnm,bhmd->bhnd', attn, v)
        return out.transpose(0, 2, 1, 3).reshape(B, N, C)

    def _L0_ffn_ref(x, ln1_w, ln2_w, c_attn_w, c_proj_w, w_g, c_fc, c_proj_e):
        import jax, jax.numpy as jnp
        import numpy as np
        import math
        N_HEAD = 12
        N_EXP = 8
        TOP_K = 2
        EVAL_CAPACITY = 1.0
        MIN_CAPACITY = 4
        EPS = 1e-05

        def layer_norm(x, w):
            mu = jnp.mean(x, axis=-1, keepdims=True)
            var = jnp.var(x, axis=-1, keepdims=True)
            return (x - mu) / jnp.sqrt(var + EPS) * w

        def attention(x, c_attn_w, c_proj_w):
            B, T, C = x.shape
            H, D = (N_HEAD, C // N_HEAD)
            qkv = x @ c_attn_w.T
            q, k, v = jnp.split(qkv, 3, axis=-1)
            q = q.reshape(B, T, H, D).transpose(0, 2, 1, 3)
            k = k.reshape(B, T, H, D).transpose(0, 2, 1, 3)
            v = v.reshape(B, T, H, D).transpose(0, 2, 1, 3)
            scores = jnp.einsum('bhqd,bhkd->bhqk', q, k) * (1.0 / math.sqrt(D))
            causal = jnp.tril(jnp.ones((T, T), dtype=bool))
            scores = jnp.where(causal, scores, -jnp.inf)
            att = jax.nn.softmax(scores, axis=-1)
            y = jnp.einsum('bhqk,bhkd->bhqd', att, v)
            y = y.transpose(0, 2, 1, 3).reshape(B, T, C)
            return y @ c_proj_w.T

        def get_capacity(num_tokens):
            cap = int(math.floor(TOP_K * EVAL_CAPACITY * num_tokens / N_EXP))
            cap += cap % 2
            return max(cap, MIN_CAPACITY)

        def moe(x_flat, w_g, c_fc, c_proj_e):
            n_tok, C = x_flat.shape
            logits = x_flat @ w_g.T
            top_vals, top_idx = jax.lax.top_k(logits, TOP_K)
            rows = jnp.arange(n_tok)[:, None]
            masked = jnp.full_like(logits, -jnp.inf).at[rows, top_idx].set(top_vals)
            probs = jax.nn.softmax(masked, axis=-1)
            cap = get_capacity(n_tok)
            flat_e = top_idx.reshape(-1)
            onehot = jax.nn.one_hot(flat_e, N_EXP, dtype=jnp.int32)
            pos = jnp.cumsum(onehot, axis=0) - onehot
            slot = jnp.take_along_axis(pos, flat_e[:, None], axis=1)[:, 0]
            valid = slot < cap
            tok = jnp.repeat(jnp.arange(n_tok), TOP_K)
            slot_c = jnp.where(valid, slot, cap)
            sec = jnp.zeros((n_tok, N_EXP, cap + 1), dtype=x_flat.dtype)
            sec = sec.at[tok, flat_e, slot_c].set(1.0)[:, :, :cap]
            w_tok = probs[tok, flat_e]
            cb = jnp.zeros((n_tok, N_EXP, cap + 1), dtype=x_flat.dtype)
            cb = cb.at[tok, flat_e, slot_c].set(w_tok)[:, :, :cap]
            dispatched = jnp.einsum('tec,td->ecd', sec, x_flat)
            h = jax.nn.gelu(jnp.einsum('ecd,edh->ech', dispatched, c_fc), approximate=False)
            out = jnp.einsum('ech,ehd->ecd', h, c_proj_e)
            return jnp.einsum('tec,ecd->td', cb, out)
        x = x + attention(layer_norm(x, ln1_w), c_attn_w, c_proj_w)
        B, T, C = x.shape
        x_ln = layer_norm(x, ln2_w)
        moe_out = moe(x_ln.reshape(B * T, C), w_g, c_fc, c_proj_e)
        return x + moe_out.reshape(B, T, C)

    def _L1_attn_ref(x, scale, w_qkv, w_proj, b_proj):
        import jax, jax.numpy as jnp
        import numpy as np
        B, N, DIM = (64, 197, 192)
        H = 12
        IN_DIM = 192
        HD = IN_DIM // H
        Bx, Nx, C = x.shape
        qkv = jnp.einsum('bnc,oc->bno', x, w_qkv).reshape(Bx, Nx, 3, H, HD)
        qkv = qkv.transpose(2, 0, 3, 1, 4)
        q, k, v = (qkv[0], qkv[1], qkv[2])
        attn = jnp.einsum('bhid,bhjd->bhij', q, k) * scale[None, :, None, None]
        diag = jnp.eye(Nx, dtype=bool)
        attn = jnp.where(diag[None, None, :, :], -jnp.inf, attn)
        attn = jax.nn.softmax(attn, axis=-1)
        out = jnp.einsum('bhij,bhjd->bhid', attn, v)
        out = out.transpose(0, 2, 1, 3).reshape(Bx, Nx, IN_DIM)
        out = out @ w_proj.T + b_proj
        return out + x

    def _L1_ffn_ref(x, attn_q, attn_k, attn_v, attn_o, ffn_wi, ffn_wo, ln1, ln2, ln_f, rel_emb, gate_w, moe_w1, moe_w2):
        import jax, jax.numpy as jnp
        import numpy as np
        B, S, D, F = (2, 128, 192, 768)
        L, H, DK = (4, 12, 64)
        E, K = (8, 2)
        NB, MAXD = (32, 128)
        MOE_LAYERS = (1, 3)
        EPS = 1e-06

        def t5_layer_norm(x, w):
            var = jnp.mean(x * x, axis=-1, keepdims=True)
            return w * x * jax.lax.rsqrt(var + EPS)

        def relative_position_bias(rel_emb, seq_len):
            ctx = jnp.arange(seq_len)[:, None]
            mem = jnp.arange(seq_len)[None, :]
            rel = mem - ctx
            nb = NB // 2
            buckets = (rel > 0).astype(jnp.int32) * nb
            n = jnp.abs(rel)
            max_exact = nb // 2
            is_small = n < max_exact
            nf = jnp.maximum(n, 1).astype(jnp.float32)
            large = max_exact + (jnp.log(nf / max_exact) / np.log(MAXD / max_exact) * (nb - max_exact)).astype(jnp.int32)
            large = jnp.minimum(large, nb - 1)
            buckets = buckets + jnp.where(is_small, n, large)
            return rel_emb[buckets].transpose(2, 0, 1)[None]

        def moe_ffn(x2d, gw, w1, w2):
            logits = x2d @ gw
            vals, idx = jax.lax.top_k(logits, K)
            gsc = jax.nn.softmax(vals, axis=-1)
            T = x2d.shape[0]
            cw = jnp.zeros((T, E), x2d.dtype).at[jnp.arange(T)[:, None], idx].add(gsc)

            def body(acc, xs):
                w1e, w2e, cwe = xs
                y = jax.nn.gelu(x2d @ w1e, approximate=False) @ w2e
                return (acc + cwe[:, None] * y, None)
            out, _ = jax.lax.scan(body, jnp.zeros_like(x2d), (w1, w2, cw.T))
            return out
        b, s, d = x.shape
        bias = relative_position_bias(rel_emb, s)
        h = x
        mi = 0
        for i in range(L):
            nx = t5_layer_norm(h, ln1[i])
            q = (nx @ attn_q[i]).reshape(b, s, H, DK)
            k = (nx @ attn_k[i]).reshape(b, s, H, DK)
            v = (nx @ attn_v[i]).reshape(b, s, H, DK)
            scores = jnp.einsum('bqhd,bkhd->bhqk', q, k) + bias
            attn = jax.nn.softmax(scores, axis=-1)
            ctx = jnp.einsum('bhqk,bkhd->bqhd', attn, v).reshape(b, s, H * DK)
            h = h + ctx @ attn_o[i]
            nx = t5_layer_norm(h, ln2[i])
            y = jax.nn.relu(nx @ ffn_wi[i]) @ ffn_wo[i]
            if i in MOE_LAYERS:
                y = y + moe_ffn(nx.reshape(-1, d), gate_w[mi], moe_w1[mi], moe_w2[mi]).reshape(b, s, d)
                mi += 1
            h = h + y
        return t5_layer_norm(h, ln_f)
    h = _L0_tok_ref(x, L0_tok_W, L0_tok_b, L0_tok_positions, L0_tok_cls_embedding)
    h = _layernorm(h + _L0_attn_ref(h, L0_attn_qkv_w, L0_attn_qkv_b, L0_attn_ln_g, L0_attn_ln_b), axis=-1)
    h = _layernorm(h + _L0_ffn_ref(h, L0_ffn_ln1_w, L0_ffn_ln2_w, L0_ffn_c_attn_w, L0_ffn_c_proj_w, L0_ffn_w_g, L0_ffn_c_fc, L0_ffn_c_proj_e), axis=-1)
    h = _layernorm(h + _L1_attn_ref(h, L1_attn_scale, L1_attn_w_qkv, L1_attn_w_proj, L1_attn_b_proj), axis=-1)
    h = _layernorm(h + _L1_ffn_ref(h, L1_ffn_attn_q, L1_ffn_attn_k, L1_ffn_attn_v, L1_ffn_attn_o, L1_ffn_ffn_wi, L1_ffn_ffn_wo, L1_ffn_ln1, L1_ffn_ln2, L1_ffn_ln_f, L1_ffn_rel_emb, L1_ffn_gate_w, L1_ffn_moe_w1, L1_ffn_moe_w2), axis=-1)
    return h

_drawn_inputs = setup_inputs


def setup_inputs(seed=0):
    import zlib

    import numpy as np

    out = dict(_drawn_inputs(seed))
    spreads = {'L0_attn_qkv_b': (0.0, 0.1),
     'L0_attn_ln_g': (1.0, 0.6),
     'L0_attn_ln_b': (0.0, 0.314),
     'L0_ffn_ln1_w': (1.0, 0.6),
     'L0_ffn_ln2_w': (1.0, 0.6),
     'L1_attn_scale': (0.25, 0.6),
     'L1_attn_b_proj': (0.0, 0.1),
     'L1_ffn_ln1': (1.0, 0.6),
     'L1_ffn_ln2': (1.0, 0.549),
     'L1_ffn_ln_f': (1.0, 0.2)}
    factors = {'L0_tok_b': 2.868,
     'L0_ffn_c_attn_w': 3.655,
     'L0_ffn_c_proj_w': 3.542,
     'L1_attn_w_qkv': 6.758,
     'L1_attn_w_proj': 6.682,
     'L1_ffn_rel_emb': 8.0}
    for name, (base, spread) in spreads.items():
        noise = np.random.default_rng([zlib.crc32(name.encode()), seed]).standard_normal(out[name].shape)
        drawn = base * np.exp(spread * noise) if base else spread * noise
        out[name] = jnp.asarray(drawn.astype(out[name].dtype))
    for name, factor in factors.items():
        out[name] = (out[name] * factor).astype(out[name].dtype)
    return out
```

```python
from contextlib import ExitStack

import numpy as np

import concourse.bass as bass
from concourse import mybir

ALU = mybir.AluOpType
ACT = mybir.ActivationFunctionType
AX = mybir.AxisListType
F32 = mybir.dt.float32
BF16 = mybir.dt.bfloat16
I32 = mybir.dt.int32
U32 = mybir.dt.uint32

B, CIN, IMGSZ, PATCH = 32, 3, 96, 16
GRID = IMGSZ // PATCH
NTOK = GRID * GRID + 1
C = 192
KC = C // 2
H = 12
IPG = 3
TG = IPG * NTOK
G = -(-B // IPG)
T = G * TG
T_REAL = B * NTOK
PD = CIN * PATCH * PATCH
PCH = PD // 128
F = 768
FC = F // 128
E = 8
TOP_K = 2
CAP = TOP_K * T_REAL // E
CAP += CAP % 2
LAYERS = 4
MOE_LAYERS = (1, 3)
NEG = -1.0e30
SMALL_D = C // H
T5_D = 64
BLOCKS = [(0, 4), (4, 4), (8, 3)]
RSQRT_SEED = 1597463007.0

NEIGH, CAUSAL, DIAG, T5 = 0, 1, 2, 3
NATT = 3 + LAYERS


class Att:

    def __init__(self, a):
        self.a = a
        self.t5 = a >= T5
        self.d = T5_D if self.t5 else SMALL_D
        self.rows = 64 if self.t5 else 32
        self.per_chunk = 128 // self.rows
        self.chunks = H // self.per_chunk
        self.items = self.chunks // 3
        self.proj = a != NEIGH
        self.pe_mask = not self.t5
        self.och = 128 if self.t5 else KC
        self.ochunks = H * self.d // self.och

    def heads(self, u):
        if self.t5:
            return [(3 * (u // 2) + c, 64 * (u % 2)) for c in range(3)]
        return [(c, 32 * u) for c in range(3)]

    def head(self, chunk, start):
        return chunk * self.per_chunk + start // self.rows


ATTS = [Att(a) for a in range(NATT)]


def stages():
    out = [("att", 0), ("att", 1), ("ffn", 0), ("att", 2)]
    for l in range(LAYERS):
        out += [("att", T5 + l), ("ffn", 1 + l)]
    return out


def ffn_runs(f):
    if f == 0:
        return list(range(E))
    return [-1] + (list(range(E)) if f - 1 in MOE_LAYERS else [])


def is_moe(f):
    return f == 0 or f - 1 in MOE_LAYERS


def att_order(a):
    s = ATTS[a]
    def qkv(g):
        return [[("Q", g, j)] for j in range(s.items)] + [[("K", g, j)] for j in range(s.items)] + \
               [[("V", g, j)] for j in range(s.items)]
    out = []
    if a == 0:
        out += [("TOK", 0), ("TOK", 1)]
    out.append(("A", 0))
    for x in qkv(0):
        out += x
    if a == 0:
        out.append(("TOK", 2))
    out.append(("A", 1))
    for g in range(G):
        fill = []
        if s.proj and g >= 1:
            fill += [[("OT", g - 1, j)] for j in range(s.items)]
        if g + 1 < G:
            fill += qkv(g + 1)
        if a == 0 and g + 3 < G:
            fill.append([("TOK", g + 3)])
        if s.proj and g >= 1:
            fill.append([("Y", g - 1)])
        if g + 2 < G:
            fill.append([("A", g + 2)])
        main = [[("S", g, 0), ("S", g, 1)], [("PT", g, 0)], [("S", g, 2)], [("PV", g, 0), ("PT", g, 1)],
                [("S", g, 3)], [("PV", g, 1), ("PT", g, 2)], [("PV", g, 2)], [("PT", g, 3)], [("PV", g, 3)]]
        gaps = [0, 2, 4, 6, 7]
        n, k = len(fill), 0
        for i, m in enumerate(main):
            out += m
            if i in gaps:
                upto = n * (gaps.index(i) + 1) // len(gaps)
                for x in fill[k:upto]:
                    out += x
                k = upto
    if s.proj:
        out += [("OT", G - 1, j) for j in range(s.items)] + [("Y", G - 1)]
    return out


def ffn_order(f):
    out = []
    for g in range(G):
        out.append(("A", g))
        if is_moe(f):
            out.append(("L", g))
    if f == 0:
        out.append(("CNT",))
    if is_moe(f):
        out.append(("GATE",))
    runs = ffn_runs(f)
    blocks = [(k, b) for k in range(len(runs)) for b in range(len(BLOCKS))]
    before = []
    for k, b in blocks:
        for m in range(FC):
            out.append(("U", k, b, m))
            if m and before:
                out.append(before.pop(0))
        before = [("D", k, g) for g in range(BLOCKS[b][0], sum(BLOCKS[b]))]
    return out + before


def order(stage):
    return att_order(stage[1]) if stage[0] == "att" else ffn_order(stage[1])


def numbered():
    proj, score, turned, ready = {}, {}, {}, {}
    every = stages()
    for st, after in zip(every, every[1:] + [None]):
        for step in order(st):
            key = (st, *step)
            if step[0] in ("TOK", "Q", "K", "V", "OT", "Y", "U"):
                proj[key] = len(proj)
            elif step[0] in ("S", "L", "CNT", "D"):
                score[key] = len(score)
            elif step[0] == "A":
                turned[key] = len(turned)
            if step[0] == "TOK":
                ready[(st, step[1])] = len(ready)
            elif after and (step[0] == "Y" or (st == ("att", NEIGH) and step[0] == "PV" and step[2] == 3)
                            or (step[0] == "D" and step[1] == len(ffn_runs(st[1])) - 1)):
                ready[(after, step[2] if step[0] == "D" else step[1])] = len(ready)
    return proj, score, turned, ready


PROJ, SCORE, TURNED, READY = numbered()
RUN0 = {0: 0}
for _f in range(LAYERS):
    RUN0[_f + 1] = RUN0[_f] + len(ffn_runs(_f))
NRUNS = RUN0[LAYERS] + len(ffn_runs(LAYERS))
FW_RING = 3
PATCH_RING = 3

K_IDENT, K_BAND, K_BLOCK, K_CAUSAL, K_DIAG, K_BEFORE, K_ONES, K_IOTA = [TG * i for i in range(8)]
K_WIDTH = 7 * TG + G * E
R_LNG, R_LNB, R_BPROJ, R_LNF, R_POS, R_TOKB = range(6)
GAIN = {("att", 1): 0, ("ffn", 0): 1}
for _l in range(LAYERS):
    GAIN[("att", T5 + _l)] = 2 + 2 * _l
    GAIN[("ffn", 1 + _l)] = 3 + 2 * _l
NGAIN = 2 + 2 * LAYERS
WG = {0: 0, 2: 1, 4: 2}
QK_SMALL = 4 * 32 * 3
AWB_W = 4 * 2 * QK_SMALL + 2 * C
AWC_W = 2 * 2 * QK_SMALL + 2 * C + 2 * C
AWE_W = 3 * 2 * F
WO_W = FC * C


def tower(nc, patches, tok_w, consts, rows, gains, gates_w, head_scale, bias_src, edge,
          aw_neigh, aw_causal, aw_diag, aw_t5, wo_t5, w1_all, w2_all, out):
    with ExitStack() as ctx:
        def sb(name, shape, dt=F32):
            return ctx.enter_context(nc.sbuf_tensor(name, shape, dt))

        def ps(name, shape):
            return ctx.enter_context(nc.psum_tensor(name, shape, F32))

        def sem(name):
            return ctx.enter_context(nc.semaphore(name))

        x = sb("x", [TG, G, C])
        held = sb("held", [TG, G, C])
        xn = sb("xn", [TG, G, C])
        xt = sb("xt", [KC + 1, 2, T])
        xband = sb("xband", [KC + 1, 2, 2, TG])
        patch = sb("patch", [128, PATCH_RING, PCH, TG])
        tokw = sb("tokw", [128, PCH, C])
        const = sb("const", [TG, K_WIDTH])
        row = sb("row", [TG, 6, C])
        gain = sb("gain", [KC, 2, NGAIN])
        gatew = sb("gatew", [KC, 2, 3, E])
        hscale = sb("hscale", [KC, QK_SMALL])
        identb = sb("identb", [TG, TG], BF16)
        maskb = sb("maskb", [TG, 3, 3, TG], BF16)
        relbias = sb("relbias", [TG, H, TG])
        aw = sb("aw", [128, 2, AWE_W])
        wo = sb("wo", [128, 2, WO_W])
        w1 = sb("w1", [KC, FW_RING, 2 * F])
        w2 = sb("w2", [128, FW_RING, FC * C])
        qt = sb("qt", [128, 2, 6, TG])
        kt = sb("kt", [128, 2, 6, TG])
        v64 = sb("v64", [TG, 2, H, T5_D + 1])
        v16 = sb("v16", [TG, 2, H, SMALL_D + 1])
        prob = sb("prob", [TG, 2, 3, TG])
        probt = sb("probt", [TG, 2, 3, TG])
        o = sb("o", [TG, 2, F])
        ot = sb("ot", [128, 2, 6, TG])
        hid = sb("hid", [128, 2, FC, 4 * TG])
        negmax = sb("negmax", [TG, 3])
        rden = sb("rden", [TG, H])
        stat = sb("stat", [TG, 6])
        mv = sb("mv", [TG, 2])
        var = sb("var", [TG, 1])
        rs = sb("rs", [TG, 1])
        tmp = sb("tmp", [TG, 1])
        wide = sb("wide", [TG, C])
        logit = sb("logit", [TG, G, E])
        best = sb("best", [TG, G, 8])
        best_at = sb("best_at", [TG, G, 8], U32)
        atf = sb("atf", [TG, G, 2])
        gap = sb("gap", [TG, G])
        egap = sb("egap", [TG, G])
        p1 = sb("p1", [TG, G])
        p2 = sb("p2", [TG, G])
        hot1 = sb("hot1", [TG, G, E])
        hot2 = sb("hot2", [TG, G, E])
        both = sb("both", [TG, G, E])
        cnt = sb("cnt", [TG, 2, G, E])
        cw = sb("cw", [TG, G, E])
        onesr = sb("onesr", [1, 2])

        ps_turn = ps("ps_turn", [128, 512])
        ps_proj = ps("ps_proj", [128, 2, 512])
        ps_score = ps("ps_score", [128, 2, 512])
        ps_pt = ps("ps_pt", [128, 512])
        ps_o = ps("ps_o", [128, 2, 512])

        const_in = sem("const_in")
        patch_in = [sem(f"patch_in{i}") for i in range(PATCH_RING)]
        aw_in = [sem(f"aw_in{i}") for i in range(2)]
        fw_in = [sem(f"fw_in{i}") for i in range(FW_RING)]
        setup_done = sem("setup_done")
        aw_scaled = sem("aw_scaled")
        xn_ready = sem("xn_ready")
        turn_full = sem("turn_full")
        xt_ready = sem("xt_ready")
        proj_full = sem("proj_full")
        proj_taken = [sem(f"proj_taken{i}") for i in range(2)]
        score_full = sem("score_full")
        score_taken = [sem(f"score_taken{i}") for i in range(2)]
        shifted = sem("shifted")
        prob_ready = sem("prob_ready")
        pt_full = sem("pt_full")
        pt_taken = sem("pt_taken")
        o_full = sem("o_full")
        o_ready = sem("o_ready")
        gap_ready = sem("gap_ready")
        egap_ready = sem("egap_ready")
        hot_ready = sem("hot_ready")
        gate_ready = sem("gate_ready")
        out_ready = sem("out_ready")
        out_done = sem("out_done")
        dve_step = sem("dve_step")

        ident = const[:, K_IDENT:K_IDENT + TG]
        band = const[:, K_BAND:K_BAND + TG]
        before_m = const[:, K_BEFORE:K_BEFORE + TG]
        ones_m = const[:, K_ONES:K_ONES + TG]
        iota = const[:, K_IOTA:K_IOTA + G * E].rearrange("p (g e) -> p g e", g=G)

        def aw_part(slot, at, n):
            return aw[:, slot, at:at + 2 * n].rearrange("p (c n) -> p c n", c=2)

        def tokens(g, n=1):
            return slice(g * TG, (g + n) * TG)

        def v_of(a):
            return v64 if ATTS[a].t5 else v16

        def unit(a, g, u):
            return (a * G + g) * 4 + u

        NCONST = 10

        def last_item(table, st):
            return max(n for key, n in table.items() if key[0] == st)

        block = ctx.enter_context(nc.Block())

        @block.sync
        def _(sp):
            for dst, src in ((const[:], consts), (tokw[:], tok_w), (row[:], rows), (gain[:], gains),
                             (gatew[:], gates_w), (hscale[:], head_scale), (relbias[:], bias_src),
                             (xband[KC:KC + 1, 0, 0, :], edge), (xband[KC:KC + 1, 1, 0, :], edge),
                             (onesr[:], consts[0:1, K_ONES:K_ONES + 2])):
                sp.dma_start(dst, src).then_inc(const_in, 16)

            def load_patch(g):
                if g >= PATCH_RING:
                    sp.wait_ge(proj_full, PROJ[(("att", 0), "TOK", g - PATCH_RING)] + 1)
                sp.dma_start(patch[:, g % PATCH_RING, :, :], patches[g]).then_inc(patch_in[g % PATCH_RING], 16)

            def load_aw(a):
                if a >= 2:
                    st = ("att", a - 2)
                    sp.wait_ge(proj_full, last_item(PROJ, st) + 1)
                src = (aw_neigh, aw_causal, aw_diag)[a] if a < T5 else aw_t5[a - T5]
                sp.dma_start(aw[0:src.shape[0], a % 2, 0:src.shape[1]], src).then_inc(aw_in[a % 2], 16)
                if a >= T5:
                    sp.dma_start(wo[:, a % 2, :], wo_t5[a - T5]).then_inc(aw_in[a % 2], 16)

            def load_fw(r):
                s = r % FW_RING
                if r >= FW_RING:
                    f = max(f for f in RUN0 if RUN0[f] <= r - FW_RING)
                    k = r - FW_RING - RUN0[f]
                    sp.wait_ge(score_full, SCORE[(("ffn", f), "D", k, G - 1)] + 1)
                sp.dma_start(w1[:, s, :], w1_all[r]).then_inc(fw_in[s], 16)
                sp.dma_start(w2[:, s, :], w2_all[r]).then_inc(fw_in[s], 16)

            for g in range(PATCH_RING):
                load_patch(g)
            load_aw(0)
            for g in range(PATCH_RING, G):
                load_patch(g)
            load_aw(1)
            for r in range(FW_RING):
                load_fw(r)
            for st in stages():
                if st[0] == "att" and st[1] + 2 < NATT:
                    load_aw(st[1] + 2)
                if st[0] == "ffn":
                    for k in range(len(ffn_runs(st[1]))):
                        if RUN0[st[1]] + k + FW_RING < NRUNS:
                            load_fw(RUN0[st[1]] + k + FW_RING)
            for g in range(G):
                n = min(TG, T_REAL - g * TG)
                sp.wait_ge(out_ready, g + 1)
                sp.dma_start(out[g * TG:g * TG + n, :], xn[0:n, g, :]).then_inc(out_done, 16)
            sp.wait_ge(out_done, 16 * G)

        @block.tensor
        def _(pe):
            def proj_bank(key):
                n = PROJ[key]
                if n >= 2:
                    pe.wait_ge(proj_taken[n % 2], n // 2)
                return ps_proj[:, n % 2, :]

            def proj_out(key):
                n = PROJ[key]
                pe.wait_ge(proj_taken[n % 2], n // 2 + 1)

            def score_bank(key):
                n = SCORE[key]
                if n >= 2:
                    pe.wait_ge(score_taken[n % 2], n // 2)
                return ps_score[:, n % 2, :]

            def turn(st, g):
                n = TURNED[(st, "A", g)]
                pe.wait_ge(xn_ready, READY[(st, g)] + 1)
                if n:
                    pe.wait_ge(xt_ready, n)
                src = x if st == ("att", DIAG) else xn
                for c in range(2):
                    last = pe.transpose(ps_turn[0:KC, c * TG:(c + 1) * TG], src[:, g, c * KC:(c + 1) * KC], ident)
                if st == ("att", NEIGH):
                    for c in range(2):
                        last = pe.matmul(ps_turn[0:KC, (2 + c) * TG:(3 + c) * TG], src[:, g, c * KC:(c + 1) * KC],
                                         band, start=True, stop=True)
                last.then_inc(turn_full, 1)

            def att_step(st, step):
                a = st[1]
                s = ATTS[a]
                kind, g = step[0], step[1]
                par = g % 2
                key = (st, *step)
                if kind == "A":
                    turn(st, g)
                elif kind == "TOK":
                    bank = proj_bank(key)
                    pe.wait_ge(patch_in[g % PATCH_RING], 16 * (g // PATCH_RING + 1))
                    for c in range(PCH):
                        last = pe.matmul(bank[0:TG, 0:C], patch[:, g % PATCH_RING, c, :], tokw[:, c, :],
                                         start=(c == 0), stop=(c == PCH - 1))
                    last.then_inc(proj_full, 1)
                elif kind in ("Q", "K"):
                    j = step[2]
                    bank = proj_bank(key)
                    pe.wait_ge(xt_ready, TURNED[(st, "A", g)] + 1)
                    width = F if s.t5 else QK_SMALL
                    which = 0 if kind == "Q" else 1
                    if a == NEIGH:
                        parts = [(aw_part(a % 2, (2 * which + i) * 2 * width, width), i) for i in range(2)]
                    else:
                        parts = [(aw_part(a % 2, which * 2 * width, width), 0)]
                    for i in range(3):
                        m = 3 * j + i
                        terms = []
                        for w, banded in parts:
                            for c in range(2):
                                k = KC + 1 if a == NEIGH and c == 0 else KC
                                src = xband[0:k, par, c, :] if banded else xt[0:k, c, tokens(g)]
                                terms.append((w[0:k, c, m * 128:(m + 1) * 128], src))
                        for n, (w, src) in enumerate(terms):
                            last = pe.matmul(bank[:, i * TG:(i + 1) * TG], w, src, start=(n == 0),
                                             stop=(n == len(terms) - 1))
                    last.then_inc(proj_full, 1)
                elif kind == "V":
                    j = step[2]
                    bank = proj_bank(key)
                    width = F if s.t5 else C
                    at = (4 if s.t5 or a != NEIGH else 8) * (F if s.t5 else QK_SMALL)
                    w = aw_part(a % 2, at, width)
                    n = width // s.items
                    for c in range(2):
                        k = KC + 1 if a == NEIGH and c == 0 else KC
                        last = pe.matmul(bank[0:TG, 0:n], xt[0:k, c, tokens(g)], w[0:k, c, j * n:(j + 1) * n],
                                         start=(c == 0), stop=(c == 1))
                    last.then_inc(proj_full, 1)
                elif kind == "S":
                    u = step[2]
                    bank = score_bank(key)
                    if u == 0:
                        for what in ("Q", "K", "V"):
                            for j in range(s.items):
                                proj_out((st, what, g, j))
                    if s.pe_mask:
                        pe.matmul(bank[0:TG, 0:3 * TG], identb[:], maskb[:, a, :, :].rearrange("p h k -> p (h k)"),
                                  start=True, stop=False, skip_group_check=True)
                    for i, (c, p) in enumerate(s.heads(u)):
                        last = pe.matmul(bank[0:TG, i * TG:(i + 1) * TG], qt[p:p + s.rows, par, c, :],
                                         kt[p:p + s.rows, par, c, :], start=not s.pe_mask, stop=True,
                                         skip_group_check=True)
                    last.then_inc(score_full, 1)
                elif kind == "PT":
                    u = step[2]
                    n = unit(a, g, u)
                    pe.wait_ge(prob_ready, n + 1)
                    if n:
                        pe.wait_ge(pt_taken, n)
                    for i in range(3):
                        last = pe.transpose(ps_pt[0:TG, i * TG:(i + 1) * TG], prob[:, u % 2, i, :], ident)
                    last.then_inc(pt_full, 1)
                elif kind == "PV":
                    u = step[2]
                    pe.wait_ge(pt_taken, unit(a, g, u) + 1)
                    if u == 0 and a * G + g:
                        pe.wait_ge(o_ready, a * G + g)
                    v = v_of(a)
                    for i, (c, p) in enumerate(s.heads(u)):
                        h = s.head(c, p)
                        at = (h % 6) * (s.d + 1)
                        last = pe.matmul(ps_o[0:TG, h // 6, at:at + s.d + 1], probt[:, u % 2, i, :], v[:, par, h, :],
                                         start=True, stop=True, skip_group_check=True)
                    if u == 3:
                        last.then_inc(o_full, 1)
                elif kind == "OT":
                    j = step[2]
                    bank = proj_bank(key)
                    pe.wait_ge(o_ready, a * G + g + 1)
                    n = s.ochunks // s.items
                    for i in range(n):
                        m = j * n + i
                        last = pe.transpose(bank[0:s.och, i * TG:(i + 1) * TG],
                                            o[:, par, m * s.och:(m + 1) * s.och], ident)
                    last.then_inc(proj_full, 1)
                elif kind == "Y":
                    bank = proj_bank(key)
                    for j in range(s.items):
                        proj_out((st, "OT", g, j))
                    if s.t5:
                        w = wo[:, a % 2, :].rearrange("p (c n) -> p c n", c=FC)
                    else:
                        w = aw_part(a % 2, 4 * QK_SMALL + 2 * C, C)
                    for c in range(s.ochunks):
                        last = pe.matmul(bank[0:TG, 0:C], ot[0:s.och, par, c, :], w[0:s.och, c, :],
                                         start=(c == 0), stop=(c == s.ochunks - 1))
                    last.then_inc(proj_full, 1)

            def ffn_step(st, step):
                f = st[1]
                kind = step[0]
                key = (st, *step)
                if kind == "A":
                    turn(st, step[1])
                elif kind == "L":
                    g = step[1]
                    bank = score_bank(key)
                    pe.wait_ge(xt_ready, TURNED[(st, "A", g)] + 1)
                    for c in range(2):
                        last = pe.matmul(bank[0:TG, 0:E], xt[0:KC, c, tokens(g)], gatew[:, c, WG[f], :],
                                         start=(c == 0), stop=(c == 1))
                    last.then_inc(score_full, 1)
                elif kind == "CNT":
                    bank = score_bank(key)
                    pe.wait_ge(hot_ready, 1)
                    rhs = both[:].rearrange("p g e -> p (g e)")
                    pe.matmul(bank[0:TG, 0:G * E], before_m, rhs, start=True, stop=True)
                    pe.matmul(bank[0:TG, G * E:2 * G * E], ones_m, rhs, start=True, stop=True).then_inc(score_full, 1)
                elif kind == "U":
                    _, k, b, m = step
                    r = RUN0[f] + k
                    slot = r % FW_RING
                    bank = proj_bank(key)
                    if m == 0 and b == 0:
                        pe.wait_ge(fw_in[slot], 32 * (r // FW_RING + 1))
                        if k == 0:
                            pe.wait_ge(xt_ready, TURNED[(st, "A", G - 1)] + 1)
                    g0, n = BLOCKS[b]
                    w = w1[:, slot, :].rearrange("p (c n) -> p c n", c=2)
                    for c in range(2):
                        last = pe.matmul(bank[:, 0:n * TG], w[:, c, m * 128:(m + 1) * 128], xt[0:KC, c, tokens(g0, n)],
                                         start=(c == 0), stop=(c == 1))
                    last.then_inc(proj_full, 1)
                elif kind == "D":
                    _, k, g = step
                    r = RUN0[f] + k
                    slot = r % FW_RING
                    bank = score_bank(key)
                    b = min(g // 4, 2)
                    if g == BLOCKS[b][0]:
                        for m in range(FC - 2, FC):
                            proj_out((st, "U", k, b, m))
                    at = (g - BLOCKS[b][0]) * TG
                    w = w2[:, slot, :].rearrange("p (c n) -> p c n", c=FC)
                    for m in range(FC):
                        last = pe.matmul(bank[0:TG, 0:C], hid[:, (3 * r + b) % 2, m, at:at + TG], w[:, m, :],
                                         start=(m == 0), stop=(m == FC - 1))
                    last.then_inc(score_full, 1)

            pe.wait_ge(const_in, 16 * NCONST)
            pe.wait_ge(setup_done, 1)
            for st in stages():
                if st[0] == "att":
                    a = st[1]
                    uses = sum(32 if b >= T5 else 16 for b in range(a % 2, a + 1, 2))
                    pe.wait_ge(aw_in[a % 2], uses)
                    if a < T5:
                        pe.wait_ge(aw_scaled, a + 1)
                for step in order(st):
                    (att_step if st[0] == "att" else ffn_step)(st, step)

        @block.scalar
        def _(act):
            def take_proj(key):
                n = PROJ[key]
                act.wait_ge(proj_full, n + 1)
                return ps_proj[:, n % 2, :], proj_taken[n % 2]

            def turned(st, g):
                n = TURNED[(st, "A", g)]
                act.wait_ge(turn_full, n + 1)
                if st in GAIN:
                    for c in range(2):
                        last = act.activation(xt[0:KC, c, tokens(g)], ps_turn[0:KC, c * TG:(c + 1) * TG], ACT.Copy,
                                              scale=gain[:, c, GAIN[st]:GAIN[st] + 1])
                else:
                    last = act.activation(xt[0:KC, :, tokens(g)],
                                          ps_turn[0:KC, 0:2 * TG].rearrange("p (c n) -> p c n", c=2), ACT.Copy)
                    if st == ("att", NEIGH):
                        last = act.activation(xband[0:KC, g % 2, :, :],
                                              ps_turn[0:KC, 2 * TG:4 * TG].rearrange("p (c n) -> p c n", c=2), ACT.Copy)
                last.then_inc(xt_ready, 1)

            act.wait_ge(const_in, 16 * NCONST)
            act.wait_ge(setup_done, 1)
            gates = 0
            for st in stages():
                for step in order(st):
                    kind = step[0]
                    key = (st, *step)
                    if kind == "A":
                        turned(st, step[1])
                    elif kind in ("Q", "K"):
                        bank, taken = take_proj(key)
                        j = step[2]
                        dst = qt if kind == "Q" else kt
                        act.activation(dst[:, step[1] % 2, 3 * j:3 * j + 3, :],
                                       bank[:, 0:3 * TG].rearrange("p (c n) -> p c n", c=3), ACT.Copy).then_inc(taken, 1)
                    elif kind == "S":
                        _, g, u = step
                        a = st[1]
                        n = SCORE[key]
                        if ATTS[a].t5:
                            act.wait_ge(shifted, unit(a - T5, g, u) + 1)
                        else:
                            act.wait_ge(score_taken[n % 2], n // 2 + 1)
                        act.activation(prob[:, u % 2, :, :], prob[:, u % 2, :, :], ACT.Exp).then_inc(prob_ready, 1)
                    elif kind == "PT":
                        _, g, u = step
                        act.wait_ge(pt_full, unit(st[1], g, u) + 1)
                        act.activation(probt[:, u % 2, :, :], ps_pt[0:TG, 0:3 * TG].rearrange("p (c n) -> p c n", c=3),
                                       ACT.Copy).then_inc(pt_taken, 1)
                    elif kind == "OT":
                        bank, taken = take_proj(key)
                        _, g, j = step
                        s = ATTS[st[1]]
                        n = s.ochunks // s.items
                        act.activation(ot[0:s.och, g % 2, j * n:(j + 1) * n, :],
                                       bank[0:s.och, 0:n * TG].rearrange("p (c n) -> p c n", c=n),
                                       ACT.Copy).then_inc(taken, 1)
                    elif kind == "GATE":
                        gates += 1
                        act.wait_ge(gap_ready, gates)
                        act.activation(egap[:], gap[:], ACT.Exp).then_inc(egap_ready, 1)
                    elif kind == "U":
                        bank, taken = take_proj(key)
                        _, k, b, m = step
                        r = RUN0[st[1]] + k
                        n = BLOCKS[b][1] * TG
                        func = ACT.Relu if ffn_runs(st[1])[k] < 0 else ACT.Gelu
                        act.activation(hid[:, (3 * r + b) % 2, m, 0:n], bank[:, 0:n], func).then_inc(taken, 1)

        @block.vector
        def _(dve):
            steps = [0]

            def link(ins):
                steps[0] += 1
                ins.then_inc(dve_step, 1)
                dve.wait_ge(dve_step, steps[0])

            def tell(ins, which, value):
                ins.then_inc(which, 1)
                dve.wait_ge(which, value)

            def stats(src):
                link(dve.bn_stats(stat[:], src))
                link(dve.bn_aggr(mv[:], stat[:]))

            def rsqrt(eps):
                link(dve.tensor_scalar(var[:], var[:], eps, None, ALU.add))
                link(dve.tensor_scalar(rs[:].bitcast(I32), var[:].bitcast(I32), -0.5, RSQRT_SEED, ALU.mult, ALU.add))
                for _ in range(3):
                    link(dve.tensor_tensor(tmp[:], rs[:], rs[:], ALU.mult))
                    link(dve.scalar_tensor_tensor(out=tmp[:], in0=tmp[:], scalar=-0.5, in1=var[:], op0=ALU.mult,
                                                  op1=ALU.mult))
                    link(dve.scalar_tensor_tensor(out=rs[:], in0=tmp[:], scalar=1.5, in1=rs[:], op0=ALU.add,
                                                  op1=ALU.mult))

            def layer_norm(dst, src, eps=1e-5):
                stats(src)
                link(dve.tensor_copy(var[:], mv[:, 1:2]))
                rsqrt(eps)
                return dve.tensor_scalar(dst, src, mv[:, 0:1], rs[:], ALU.subtract, ALU.mult)

            def rms_norm(dst, src, eps=1e-6):
                stats(src)
                link(dve.scalar_tensor_tensor(out=var[:], in0=mv[:, 0:1], scalar=mv[:, 0:1], in1=mv[:, 1:2],
                                              op0=ALU.mult, op1=ALU.add))
                rsqrt(eps)
                return dve.tensor_scalar(dst, src, rs[:], None, ALU.mult)

            def take_proj(key):
                n = PROJ[key]
                dve.wait_ge(proj_full, n + 1)
                return ps_proj[:, n % 2, :], proj_taken[n % 2], n // 2 + 1

            def take_score(key):
                n = SCORE[key]
                dve.wait_ge(score_full, n + 1)
                return ps_score[:, n % 2, :], score_taken[n % 2], n // 2 + 1

            def softmax_shift(st, step, t5_units):
                a, (_, g, u) = st[1], step
                bank, taken, value = take_score((st, *step))
                scores = bank[0:TG, 0:3 * TG].rearrange("p (h k) -> p h k", h=3)
                dst = prob[:, u % 2, :, :]
                if ATTS[a].t5:
                    tell(dve.tensor_tensor(dst, scores, relbias[:, 3 * u:3 * u + 3, :], ALU.add), taken, value)
                    scores = dst
                link(dve.tensor_reduce(negmax[:], scores, AX.X, ALU.max, negate=True))
                ins = dve.tensor_tensor(dst, scores, negmax[:].unsqueeze(2).to_broadcast([TG, 3, TG]), ALU.add)
                if ATTS[a].t5:
                    tell(ins, shifted, unit(a - T5, g, u) + 1)
                else:
                    tell(ins, taken, value)

            def divide(a, g):
                s = ATTS[a]
                dve.wait_ge(o_full, a * G + g + 1)
                n = 6 * (s.d + 1)
                view = ps_o[0:TG, :, 0:n].rearrange("p b (h d) -> p b h d", h=6)
                link(dve.reciprocal(rden[:].rearrange("p (b h) -> p b h", b=2), view[:, :, :, s.d]))
                for b in range(2):
                    ins = dve.tensor_tensor(
                        o[:, g % 2, b * 6 * s.d:(b + 1) * 6 * s.d].rearrange("p (h d) -> p h d", h=6),
                        view[:, b, :, 0:s.d],
                        rden[:, 6 * b:6 * b + 6].unsqueeze(2).to_broadcast([TG, 6, s.d]), ALU.mult)
                    if b == 0:
                        link(ins)
                tell(ins, o_ready, a * G + g + 1)

            def turn_number(st, g):
                return READY[(st, g)] + 1

            def after_ffn(f, g):
                if f == 0:
                    link(dve.tensor_tensor(wide[:], held[:, g, :], x[:, g, :], ALU.add))
                    tell(layer_norm(x[:, g, :], wide[:]), xn_ready, turn_number(("att", DIAG), g))
                elif f < LAYERS:
                    tell(rms_norm(xn[:, g, :], x[:, g, :]), xn_ready, turn_number(("att", T5 + f), g))
                else:
                    link(rms_norm(wide[:], x[:, g, :]))
                    link(dve.tensor_tensor(wide[:], wide[:], row[:, R_LNF, :], ALU.mult))
                    link(dve.tensor_tensor(wide[:], wide[:], held[:, g, :], ALU.add))
                    tell(layer_norm(xn[:, g, :], wide[:]), out_ready, g + 1)

            dve.wait_ge(const_in, 16 * NCONST)
            link(dve.tensor_copy(identb[:], ident))
            for a, at in enumerate((K_BLOCK, K_CAUSAL, K_DIAG)):
                for i in range(3):
                    link(dve.tensor_copy(maskb[:, a, i, :], const[:, at:at + TG]))
            link(dve.tensor_tensor(relbias[:], relbias[:],
                                   const[:, K_BLOCK:K_BLOCK + TG].unsqueeze(1).to_broadcast([TG, H, TG]), ALU.add))
            link(dve.memset(v64[:], 1.0))
            link(dve.memset(v16[:], 1.0))
            link(dve.memset(xt[KC:KC + 1, 0, :], 1.0))
            link(dve.tensor_tensor(row[:, R_POS, :], row[:, R_POS, :], row[:, R_TOKB, :], ALU.add))
            tell(dve.memset(tmp[:], 0.0), setup_done, 1)

            def scale_weights(a):
                dve.wait_ge(aw_in[a % 2], 16 * (a // 2 + 1))
                n = 2 * QK_SMALL
                k = KC + 1 if a == NEIGH else KC
                if a == NEIGH:
                    s = float(SMALL_D) ** -0.5
                    link(dve.tensor_scalar(aw[0:k, 0, 0:n], aw[0:k, 0, 0:n], 1.2 * s, None, ALU.mult))
                    ins = dve.tensor_scalar(aw[0:k, 0, n:2 * n], aw[0:k, 0, n:2 * n], -0.2 * s, None, ALU.mult)
                elif a == CAUSAL:
                    ins = dve.tensor_scalar(aw[0:k, 1, 0:n], aw[0:k, 1, 0:n], float(SMALL_D) ** -0.5, None, ALU.mult)
                else:
                    w = aw_part(0, 0, QK_SMALL)[0:k]
                    ins = dve.tensor_tensor(w, w, hscale[:].unsqueeze(1).to_broadcast([k, 2, QK_SMALL]), ALU.mult)
                tell(ins, aw_scaled, a + 1)

            gates = 0
            for st in stages():
                if st[0] == "att" and st[1] < T5:
                    scale_weights(st[1])
                for step in order(st):
                    kind = step[0]
                    key = (st, *step)
                    if kind == "TOK":
                        g = step[1]
                        bank, taken, value = take_proj(key)
                        tell(dve.tensor_tensor(x[:, g, :], bank[0:TG, 0:C], row[:, R_POS, :], ALU.add), taken, value)
                        link(layer_norm(xn[:, g, :], x[:, g, :]))
                        link(dve.tensor_tensor(xn[:, g, :], xn[:, g, :], row[:, R_LNG, :], ALU.mult))
                        tell(dve.tensor_tensor(xn[:, g, :], xn[:, g, :], row[:, R_LNB, :], ALU.add),
                             xn_ready, turn_number(st, g))
                    elif kind == "V":
                        _, g, j = step
                        bank, taken, value = take_proj(key)
                        s = ATTS[st[1]]
                        hs = H // s.items
                        tell(dve.tensor_copy(v_of(st[1])[:, g % 2, j * hs:(j + 1) * hs, 0:s.d],
                                             bank[0:TG, 0:hs * s.d].rearrange("p (h d) -> p h d", h=hs)), taken, value)
                    elif kind == "S":
                        softmax_shift(st, step, 0)
                    elif kind == "PV" and step[2] == 3:
                        g = step[1]
                        divide(st[1], g)
                        if st[1] == NEIGH:
                            link(dve.tensor_tensor(wide[:], o[:, g % 2, 0:C], x[:, g, :], ALU.add))
                            link(layer_norm(x[:, g, :], wide[:]))
                            link(dve.tensor_copy(held[:, g, :], x[:, g, :]))
                            tell(layer_norm(xn[:, g, :], x[:, g, :]), xn_ready, turn_number(("att", CAUSAL), g))
                    elif kind == "Y":
                        g, a = step[1], st[1]
                        bank, taken, value = take_proj(key)
                        y = bank[0:TG, 0:C]
                        if a == DIAG:
                            tell(dve.scalar_tensor_tensor(out=wide[:], in0=x[:, g, :], scalar=2.0, in1=y, op0=ALU.mult,
                                                          op1=ALU.add), taken, value)
                            link(dve.tensor_tensor(wide[:], wide[:], row[:, R_BPROJ, :], ALU.add))
                            link(layer_norm(x[:, g, :], wide[:]))
                            link(dve.tensor_copy(held[:, g, :], x[:, g, :]))
                            tell(rms_norm(xn[:, g, :], x[:, g, :]), xn_ready, turn_number(("att", T5), g))
                        else:
                            tell(dve.tensor_tensor(x[:, g, :], y, x[:, g, :], ALU.add), taken, value)
                            norm = layer_norm if a == CAUSAL else rms_norm
                            f = 0 if a == CAUSAL else a - T5 + 1
                            tell(norm(xn[:, g, :], x[:, g, :]), xn_ready, turn_number(("ffn", f), g))
                    elif kind == "L":
                        g = step[1]
                        bank, taken, value = take_score(key)
                        tell(dve.tensor_copy(logit[:, g, :], bank[0:TG, 0:E]), taken, value)
                        link(dve.max(best[:, g, :], logit[:, g, :]))
                        link(dve.max_index(best_at[:, g, :], best[:, g, :], logit[:, g, :]))
                        if g == G - 1:
                            link(dve.tensor_copy(atf[:], best_at[:, :, 0:2]))
                            for k, hot in enumerate((hot1, hot2)):
                                link(dve.tensor_tensor(hot[:], iota, atf[:, :, k:k + 1].to_broadcast([TG, G, E]),
                                                       ALU.is_equal))
                            if st[1] == 0:
                                tell(dve.tensor_tensor(both[:], hot1[:], hot2[:], ALU.add), hot_ready, 1)
                    elif kind == "CNT":
                        bank, taken, value = take_score(key)
                        tell(dve.tensor_copy(cnt[:].rearrange("p a g e -> p (a g e)"), bank[0:TG, 0:2 * G * E]),
                             taken, value)
                        for g in range(1, G - 1):
                            link(dve.tensor_tensor(cnt[:, 1, g, :], cnt[:, 1, g, :], cnt[:, 1, g - 1, :], ALU.add))
                        link(dve.tensor_tensor(cnt[:, 0, 1:G, :], cnt[:, 0, 1:G, :], cnt[:, 1, 0:G - 1, :], ALU.add))
                    elif kind == "GATE":
                        gates += 1
                        tell(dve.tensor_tensor(gap[:], best[:, :, 1], best[:, :, 0], ALU.subtract), gap_ready, gates)
                        dve.wait_ge(egap_ready, gates)
                        link(dve.tensor_scalar(p1[:], egap[:], 1.0, None, ALU.add))
                        link(dve.reciprocal(p1[:], p1[:]))
                        link(dve.tensor_tensor(p2[:], p1[:], egap[:], ALU.mult))
                        link(dve.tensor_tensor(hot1[:], hot1[:], p1[:].unsqueeze(2).to_broadcast([TG, G, E]), ALU.mult))
                        link(dve.tensor_tensor(hot2[:], hot2[:], p2[:].unsqueeze(2).to_broadcast([TG, G, E]), ALU.mult))
                        link(dve.tensor_tensor(cw[:], hot1[:], hot2[:], ALU.add))
                        if st[1] == 0:
                            link(dve.scalar_tensor_tensor(
                                out=cw[:].rearrange("p g e -> p (g e)"),
                                in0=cnt[:, 0, :, :].rearrange("p g e -> p (g e)"), scalar=float(CAP),
                                in1=cw[:].rearrange("p g e -> p (g e)"), op0=ALU.is_lt, op1=ALU.mult))
                    elif kind == "D":
                        _, k, g = step
                        f = st[1]
                        runs = ffn_runs(f)
                        bank, taken, value = take_score(key)
                        e = runs[k]
                        if e < 0:
                            ins = dve.tensor_tensor(x[:, g, :], bank[0:TG, 0:C], x[:, g, :], ALU.add)
                        else:
                            ins = dve.scalar_tensor_tensor(out=x[:, g, :], in0=bank[0:TG, 0:C],
                                                           scalar=cw[:, g, e:e + 1], in1=x[:, g, :], op0=ALU.mult,
                                                           op1=ALU.add)
                        tell(ins, taken, value)
                        if k == len(runs) - 1:
                            after_ffn(f, g)


def lay_out(inp):
    f = {k: np.asarray(v) for k, v in inp.items()}
    x = f["x"]
    z = np.zeros((G * IPG, NTOK, PD), np.float32)
    p = x.reshape(B, CIN, GRID, PATCH, GRID, PATCH).transpose(0, 2, 4, 1, 3, 5).reshape(B, GRID * GRID, PD)
    z[:B, 1:] = p
    patches = z.reshape(G, TG, PCH, 128).transpose(0, 3, 2, 1)

    def chunks(w, k):
        return w.reshape(-1, k, w.shape[-1]).transpose(1, 0, 2)

    def flat(w):
        return w.reshape(w.shape[0], -1)

    t = np.arange(TG)
    same = (t[:, None] // NTOK) == (t[None, :] // NTOK)
    const = np.zeros((TG, K_WIDTH), np.float32)
    const[:, K_IDENT:K_IDENT + TG] = np.eye(TG)
    const[:, K_BAND:K_BAND + TG] = same & (abs(t[:, None] - t[None, :]) <= 1)
    const[:, K_BLOCK:K_BLOCK + TG] = np.where(same, 0.0, NEG)
    const[:, K_CAUSAL:K_CAUSAL + TG] = np.where(same & (t[:, None] >= t[None, :]), 0.0, NEG)
    const[:, K_DIAG:K_DIAG + TG] = np.where(same & (t[:, None] != t[None, :]), 0.0, NEG)
    const[:, K_BEFORE:K_BEFORE + TG] = t[:, None] < t[None, :]
    const[:, K_ONES:K_ONES + TG] = 1.0
    const[:, K_IOTA:] = np.tile(np.arange(E), G)
    edge = np.where((t % NTOK == 0) | (t % NTOK == NTOK - 1), 2.0, 3.0).astype(np.float32)[None]

    rows = np.zeros((TG, 6, C), np.float32)
    rows[:, R_LNG] = f["L0_attn_ln_g"]
    rows[:, R_LNB] = f["L0_attn_ln_b"]
    rows[:, R_BPROJ] = f["L1_attn_b_proj"]
    rows[:, R_LNF] = f["L1_ffn_ln_f"]
    pos = f["L0_tok_positions"]
    ih = np.arange(GRID) * pos.shape[2] // GRID
    pos = pos[0][:, ih][:, :, ih].reshape(C, GRID * GRID).T
    for i in range(IPG):
        rows[i * NTOK, R_POS] = f["L0_tok_cls_embedding"][0, 0]
        rows[i * NTOK + 1:(i + 1) * NTOK, R_POS] = pos
        rows[i * NTOK + 1:(i + 1) * NTOK, R_TOKB] = f["L0_tok_b"]

    gains = np.zeros((NGAIN, C), np.float32)
    gains[0], gains[1] = f["L0_ffn_ln1_w"], f["L0_ffn_ln2_w"]
    gains[2::2], gains[3::2] = f["L1_ffn_ln1"], f["L1_ffn_ln2"]
    gains = gains.reshape(NGAIN, 2, KC).transpose(2, 1, 0)
    gw = np.stack([f["L0_ffn_w_g"].T, f["L1_ffn_gate_w"][0], f["L1_ffn_gate_w"][1]])
    gw = gw.reshape(3, 2, KC, E).transpose(2, 1, 0, 3)
    hs = np.broadcast_to(np.repeat(f["L1_attn_scale"], 32)[None], (KC, QK_SMALL))

    rel = np.arange(NTOK)[None, :] - np.arange(NTOK)[:, None]
    nb, maxd = f["L1_ffn_rel_emb"].shape[0] // 2, 128
    n = np.abs(rel)
    me = nb // 2
    nf = np.maximum(n, 1).astype(np.float32)
    large = me + (np.log(nf / np.float32(me)) / np.float32(np.log(maxd / me)) * np.float32(nb - me)).astype(np.int32)
    buckets = (rel > 0) * nb + np.where(n < me, n, np.minimum(large, nb - 1))
    heads = [ATTS[T5].head(c, s) for u in range(4) for c, s in ATTS[T5].heads(u)]
    bias = np.zeros((TG, H, TG), np.float32)
    for i in range(IPG):
        sl = slice(i * NTOK, (i + 1) * NTOK)
        bias[sl, :, sl] = f["L1_ffn_rel_emb"][buckets].transpose(0, 2, 1)[:, heads]

    def spread(w, at):
        out = np.zeros((w.shape[0], H, 32), np.float32)
        out[:, :, at:at + SMALL_D] = w.reshape(-1, H, SMALL_D)
        return out.reshape(-1, QK_SMALL)

    def with_bias(w, b):
        out = np.zeros((KC + 1, 2, w.shape[1]), np.float32)
        out[:KC] = chunks(w, KC)
        out[KC, 0] = b
        return flat(out)

    w, b = f["L0_attn_qkv_w"].T, f["L0_attn_qkv_b"][None]
    aw_neigh = np.concatenate(
        [with_bias(spread(w[:, i * C:(i + 1) * C], at), spread(b[:, i * C:(i + 1) * C], at)[0])
         for i in range(2) for at in (0, SMALL_D)] + [with_bias(w[:, 2 * C:], b[0, 2 * C:])], 1)

    def small(w, wo):
        w = w.T
        return np.concatenate([flat(chunks(spread(w[:, i * C:(i + 1) * C], 0), KC)) for i in range(2)]
                              + [flat(chunks(w[:, 2 * C:], KC)), flat(chunks(wo.T, KC))], 1)

    aw_causal = small(f["L0_ffn_c_attn_w"], f["L0_ffn_c_proj_w"])
    aw_diag = small(f["L1_attn_w_qkv"], f["L1_attn_w_proj"])
    aw_t5 = np.stack([np.concatenate([flat(chunks(f[f"L1_ffn_attn_{n}"][l], KC)) for n in "qkv"], 1)
                      for l in range(LAYERS)])
    wo_t5 = np.stack([flat(chunks(f["L1_ffn_attn_o"][l], 128)) for l in range(LAYERS)])
    up, down = list(f["L0_ffn_c_fc"]), list(f["L0_ffn_c_proj_e"])
    for l in range(LAYERS):
        up.append(f["L1_ffn_ffn_wi"][l])
        down.append(f["L1_ffn_ffn_wo"][l])
        if l in MOE_LAYERS:
            up += list(f["L1_ffn_moe_w1"][MOE_LAYERS.index(l)])
            down += list(f["L1_ffn_moe_w2"][MOE_LAYERS.index(l)])
    w1 = np.stack([flat(chunks(w, KC)) for w in up])
    w2 = np.stack([flat(chunks(w, 128)) for w in down])
    out = [patches, chunks(f["L0_tok_W"], 128), const, rows, gains, gw, hs, bias, edge,
           aw_neigh, aw_causal, aw_diag, aw_t5, wo_t5, w1, w2]
    return [np.ascontiguousarray(a, dtype=np.float32) for a in out]


def kernel(**inputs):
    import concourse.bacc as bacc
    from concourse.bass_utils import run_bass_kernel_spmd

    nc = bacc.Bacc("TRN2", target_bir_lowering=False, num_devices=1)
    names = ["patches", "tok_w", "consts", "rows", "gains", "gates_w", "head_scale", "bias_src", "edge", "aw_neigh",
             "aw_causal", "aw_diag", "aw_t5", "wo_t5", "w1_all", "w2_all"]
    arrays = {n + "_dram": a for n, a in zip(names, lay_out(inputs))}
    args = [nc.dram_tensor(n, a.shape, F32, kind="ExternalInput").ap() for n, a in arrays.items()]
    out = nc.dram_tensor("out_dram", (T_REAL, C), F32, kind="ExternalOutput").ap()
    tower(nc, *args, out)
    r = run_bass_kernel_spmd(nc, [arrays], core_ids=[0])
    return r.results[0]["out_dram"].reshape(B, NTOK, C)
```

```python
from contextlib import ExitStack

import numpy as np

import concourse.bass as bass
from concourse import mybir

ALU = mybir.AluOpType
ACT = mybir.ActivationFunctionType
AX = mybir.AxisListType
F32 = mybir.dt.float32
BF16 = mybir.dt.bfloat16
I32 = mybir.dt.int32
U32 = mybir.dt.uint32

B, CIN, IMGSZ, PATCH = 32, 3, 96, 16
GRID = IMGSZ // PATCH
NTOK = GRID * GRID + 1
C = 192
KC = C // 2
H = 12
IPG = 3
TG = IPG * NTOK
G = -(-B // IPG)
T = G * TG
T_REAL = B * NTOK
PD = CIN * PATCH * PATCH
PCH = PD // 128
F = 768
FC = F // 128
E = 8
TOP_K = 2
CAP = TOP_K * T_REAL // E
CAP += CAP % 2
LAYERS = 4
MOE_LAYERS = (1, 3)
NEG = -1.0e30
LN_EPS, RMS_EPS = 1e-5, 1e-6
SMALL_D = C // H
T5_D = 64
BLOCKS = [(0, 4), (4, 4), (8, 3)]
RSQRT_SEED = 1597463007.0

NEIGH, CAUSAL, DIAG, T5 = 0, 1, 2, 3
NATT = 3 + LAYERS


class Att:

    def __init__(self, a):
        self.a = a
        self.t5 = a >= T5
        self.d = T5_D if self.t5 else SMALL_D
        self.rows = 64 if self.t5 else 32
        self.per_chunk = 128 // self.rows
        self.chunks = H // self.per_chunk
        self.items = self.chunks // 3
        self.proj = a != NEIGH
        self.pe_mask = not self.t5
        self.och = 128 if self.t5 else KC
        self.ochunks = H * self.d // self.och

    def heads(self, u):
        if self.t5:
            return [(3 * (u // 2) + c, 64 * (u % 2)) for c in range(3)]
        return [(c, 32 * u) for c in range(3)]

    def head(self, chunk, start):
        return chunk * self.per_chunk + start // self.rows


ATTS = [Att(a) for a in range(NATT)]


def stages():
    out = [("att", 0), ("att", 1), ("ffn", 0), ("att", 2)]
    for l in range(LAYERS):
        out += [("att", T5 + l), ("ffn", 1 + l)]
    return out


def ffn_runs(f):
    if f == 0:
        return list(range(E))
    return [-1] + (list(range(E)) if f - 1 in MOE_LAYERS else [])


def is_moe(f):
    return f == 0 or f - 1 in MOE_LAYERS


def att_order(a):
    s = ATTS[a]
    def qkv(g):
        return [[("Q", g, j)] for j in range(s.items)] + [[("K", g, j)] for j in range(s.items)] + \
               [[("V", g, j)] for j in range(s.items)]
    out = []
    if a == 0:
        out += [("TOK", 0), ("TOK", 1)]
    out.append(("A", 0))
    for x in qkv(0):
        out += x
    if a == 0:
        out.append(("TOK", 2))
    out.append(("A", 1))
    units = 4 * G
    for n in range(units + 3):
        g, u = divmod(n, 4)
        if u == 0:
            fill = []
            if s.proj and 2 <= g:
                fill += [[("OT", g - 2, j)] for j in range(s.items)]
            if a == 0 and g + 3 < G:
                fill.append([("TOK", g + 3)])
            more = qkv(g + 1) if g + 1 < G else []
            fill += more[:len(more) // 2]
            if s.proj and 2 <= g:
                fill.append([("Y", g - 2)])
            fill += more[len(more) // 2:]
            if a in (NEIGH, DIAG) and g >= 3:
                fill.append([("N2", g - 3)])
            if g + 2 < G:
                fill.append([("A", g + 2)])
            count, given, gap = len(fill), 0, 0
        steps = []
        if n < units:
            steps.append([("S", g, u)])
        if 1 <= n <= units:
            steps.append([("E", (n - 1) // 4, (n - 1) % 4)])
        if 2 <= n < units + 2:
            steps.append([("PT", (n - 2) // 4, (n - 2) % 4)])
        if 3 <= n:
            steps.append([("PV", (n - 3) // 4, (n - 3) % 4)])
        gaps = 4 * len(steps)
        for x in steps:
            out += x
            if x[0][0] == "E":
                continue
            gap += 1
            upto = -(-count * gap // 12)
            for y in fill[given:upto]:
                out += y
            given = max(given, min(upto, count))
        if u == 3:
            for y in fill[given:]:
                out += y
            given = count
    for y in fill[given:]:
        out += y
    last = [G - 2, G - 1] if s.proj else []
    if s.proj and ("Y", G - 2) in out:
        last = [G - 1]
    for g in last:
        out += [("OT", g, j) for j in range(s.items)] + [("Y", g)]
    if a in (NEIGH, DIAG):
        out += [("N2", g) for g in range(G) if ("N2", g) not in out]
    return out


def ffn_order(f):
    out = []
    runs = ffn_runs(f)
    before = []
    for k in range(len(runs)):
        for b, (g0, n) in enumerate(BLOCKS):
            if k == 0 and not (f == 0 and b == 2):
                for g in range(g0, g0 + n):
                    out.append(("A", g))
                    if f == 0:
                        out.append(("L", g))
            if f == 0 and (k, b) == (0, 1):
                out += [("U", k, b, m) for m in range(FC)]
                for g in range(BLOCKS[2][0], G):
                    out += [("A", g), ("L", g)]
                out += [("CNT",), ("GATE",)] + before
                before = [("D", k, g) for g in range(g0, g0 + n)]
                continue
            for m in range(FC):
                out.append(("U", k, b, m))
                if m and before:
                    out.append(before.pop(0))
            out += before
            before = [("D", k, g) for g in range(g0, g0 + n)]
            if f and is_moe(f) and (k, b) == (0, 2):
                out += [("L", g) for g in range(G)] + [("GATE",)]
    out += before
    if f == LAYERS:
        out += [("N2", g) for g in range(G)]
    return out


def order(stage):
    return att_order(stage[1]) if stage[0] == "att" else ffn_order(stage[1])


def numbered():
    proj, score, turned, ready, norms = {}, {}, {}, {}, {}
    every = stages()
    for st, after in zip(every, every[1:] + [None]):
        for step in order(st):
            key = (st, *step)
            if step[0] in ("TOK", "Q", "K", "V", "OT", "Y", "U"):
                proj[key] = len(proj)
            elif step[0] in ("S", "L", "CNT", "D"):
                score[key] = len(score)
            elif step[0] == "A":
                turned[key] = len(turned)
            if step[0] in ("TOK", "Y", "N2") or (st == ("att", NEIGH) and step[0] == "PV" and step[2] == 3) \
                    or (step[0] == "D" and step[1] == len(ffn_runs(st[1])) - 1):
                g = step[2] if step[0] == "D" else step[1]
                norms[(st, step[0], g)] = len(norms)
                ready[(st if step[0] == "TOK" else after, g)] = len(norms) - 1
    return proj, score, turned, ready, norms


PROJ, SCORE, TURNED, READY, NORMS = numbered()
NORM_RING = 6
RUN0 = {0: 0}
for _f in range(LAYERS):
    RUN0[_f + 1] = RUN0[_f] + len(ffn_runs(_f))
NRUNS = RUN0[LAYERS] + len(ffn_runs(LAYERS))
FW_RING = 2
PATCH_RING = 3

K_IDENT, K_BAND, K_BLOCK, K_CAUSAL, K_DIAG, K_BEFORE, K_ONES, K_IOTA = [TG * i for i in range(8)]
K_WIDTH = 7 * TG + G * E
R_LNG, R_LNB, R_BPROJ, R_LNF, R_POS, R_TOKB = range(6)
GAIN = {("att", 1): 0, ("ffn", 0): 1}
for _l in range(LAYERS):
    GAIN[("att", T5 + _l)] = 2 + 2 * _l
    GAIN[("ffn", 1 + _l)] = 3 + 2 * _l
NGAIN = 2 + 2 * LAYERS
WG = {0: 0, 2: 1, 4: 2}
QK_SMALL = 4 * 32 * 3
AWB_W = 4 * 2 * QK_SMALL + 2 * C
AWC_W = 2 * 2 * QK_SMALL + 2 * C + 2 * C
AWE_W = 3 * 2 * F
WO_W = FC * C


def tower(nc, patches, tok_w, consts, rows, gains, gates_w, head_scale, bias_src, edge,
          aw_neigh, aw_causal, aw_diag, aw_t5, wo_t5, w1_all, w2_all, out):
    with ExitStack() as ctx:
        def sb(name, shape, dt=F32):
            return ctx.enter_context(nc.sbuf_tensor(name, shape, dt))

        def ps(name, shape):
            return ctx.enter_context(nc.psum_tensor(name, shape, F32))

        def sem(name):
            return ctx.enter_context(nc.semaphore(name))

        x = sb("x", [TG, G, C])
        held = sb("held", [TG, G, C])
        xn = sb("xn", [TG, G, C])
        xt = sb("xt", [KC + 1, 2, T])
        xband = sb("xband", [KC + 1, 2, 2, TG])
        patch = sb("patch", [128, PATCH_RING, PCH, TG])
        tokw = sb("tokw", [128, PCH, C])
        const = sb("const", [TG, K_WIDTH])
        row = sb("row", [TG, 6, C])
        gain = sb("gain", [KC, 2, NGAIN])
        gatew = sb("gatew", [KC, 2, 3, E])
        hscale = sb("hscale", [KC, QK_SMALL])
        identb = sb("identb", [TG, TG], BF16)
        maskb = sb("maskb", [TG, 3, 3, TG], BF16)
        relbias = sb("relbias", [TG, H, TG])
        aw = sb("aw", [128, 2, AWE_W])
        wo = sb("wo", [128, 2, WO_W])
        w1 = sb("w1", [KC, FW_RING, 2 * F])
        w2 = sb("w2", [128, FW_RING, FC * C])
        qt = sb("qt", [128, 2, 6, TG])
        kt = sb("kt", [128, 2, 6, TG])
        v64 = sb("v64", [TG, 3, H, T5_D + 1])
        v16 = sb("v16", [TG, 3, H, SMALL_D + 1])
        prob = sb("prob", [TG, 3, 3, TG])
        probt = sb("probt", [TG, 2, 3, TG])
        o = sb("o", [TG, 2, F])
        ot = sb("ot", [128, 2, 6, TG])
        hid = sb("hid", [128, 2, FC, 4 * TG])
        negmax = sb("negmax", [TG, 3])
        rden = sb("rden", [TG, H])
        stat = sb("stat", [TG, 6])
        mv = sb("mv", [TG, NORM_RING, 2])
        var = sb("var", [TG, NORM_RING])
        rs = sb("rs", [TG, NORM_RING])
        tmp = sb("tmp", [TG, 2])
        wide = sb("wide", [TG, NORM_RING, C])
        logit = sb("logit", [TG, G, E])
        best = sb("best", [TG, G, 8])
        best_at = sb("best_at", [TG, G, 8], U32)
        atf = sb("atf", [TG, G, 2])
        gap = sb("gap", [TG, G])
        egap = sb("egap", [TG, G])
        p1 = sb("p1", [TG, G])
        p2 = sb("p2", [TG, G])
        hot1 = sb("hot1", [TG, G, E])
        hot2 = sb("hot2", [TG, G, E])
        both = sb("both", [TG, G, E])
        cnt = sb("cnt", [TG, 2, G, E])
        cw = sb("cw", [TG, G, E])
        onesr = sb("onesr", [1, 2])

        ps_turn = ps("ps_turn", [128, 512])
        ps_proj = ps("ps_proj", [128, 2, 512])
        ps_score = ps("ps_score", [128, 2, 512])
        ps_pt = ps("ps_pt", [128, 512])
        ps_o = ps("ps_o", [128, 2, 512])

        const_in = sem("const_in")
        patch_in = [sem(f"patch_in{i}") for i in range(PATCH_RING)]
        aw_in = [sem(f"aw_in{i}") for i in range(2)]
        fw_in = [sem(f"fw_in{i}") for i in range(FW_RING)]
        setup_done = sem("setup_done")
        aw_scaled = sem("aw_scaled")
        stats_ready = sem("stats_ready")
        norm_done = sem("norm_done")
        pool_step = sem("pool_step")
        turn_full = sem("turn_full")
        xt_ready = sem("xt_ready")
        proj_full = sem("proj_full")
        proj_taken = [sem(f"proj_taken{i}") for i in range(2)]
        score_full = sem("score_full")
        score_taken = [sem(f"score_taken{i}") for i in range(2)]
        shifted = sem("shifted")
        prob_ready = sem("prob_ready")
        pt_full = sem("pt_full")
        pt_taken = sem("pt_taken")
        o_full = sem("o_full")
        o_ready = sem("o_ready")
        gap_ready = sem("gap_ready")
        egap_ready = sem("egap_ready")
        hot_ready = sem("hot_ready")
        gate_ready = sem("gate_ready")
        out_done = sem("out_done")
        dve_step = sem("dve_step")

        ident = const[:, K_IDENT:K_IDENT + TG]
        band = const[:, K_BAND:K_BAND + TG]
        before_m = const[:, K_BEFORE:K_BEFORE + TG]
        ones_m = const[:, K_ONES:K_ONES + TG]
        iota = const[:, K_IOTA:K_IOTA + G * E].rearrange("p (g e) -> p g e", g=G)

        def aw_part(slot, at, n):
            return aw[:, slot, at:at + 2 * n].rearrange("p (c n) -> p c n", c=2)

        def tokens(g, n=1):
            return slice(g * TG, (g + n) * TG)

        def v_of(a):
            return v64 if ATTS[a].t5 else v16

        def unit(a, g, u):
            return (a * G + g) * 4 + u

        NCONST = 10

        def last_item(table, st):
            return max(n for key, n in table.items() if key[0] == st)

        block = ctx.enter_context(nc.Block())

        @block.sync
        def _(sp):
            for dst, src in ((const[:], consts), (tokw[:], tok_w), (row[:], rows), (gain[:], gains),
                             (gatew[:], gates_w), (hscale[:], head_scale), (relbias[:], bias_src),
                             (xband[KC:KC + 1, 0, 0, :], edge), (xband[KC:KC + 1, 1, 0, :], edge),
                             (onesr[:], consts[0:1, K_ONES:K_ONES + 2])):
                sp.dma_start(dst, src).then_inc(const_in, 16)

            def load_patch(g):
                if g >= PATCH_RING:
                    sp.wait_ge(proj_full, PROJ[(("att", 0), "TOK", g - PATCH_RING)] + 1)
                sp.dma_start(patch[:, g % PATCH_RING, :, :], patches[g]).then_inc(patch_in[g % PATCH_RING], 16)

            def load_aw(a):
                if a >= 2:
                    st = ("att", a - 2)
                    sp.wait_ge(proj_full, last_item(PROJ, st) + 1)
                src = (aw_neigh, aw_causal, aw_diag)[a] if a < T5 else aw_t5[a - T5]
                sp.dma_start(aw[0:src.shape[0], a % 2, 0:src.shape[1]], src).then_inc(aw_in[a % 2], 16)
                if a >= T5:
                    sp.dma_start(wo[:, a % 2, :], wo_t5[a - T5]).then_inc(aw_in[a % 2], 16)

            def load_fw(r):
                s = r % FW_RING
                if r >= FW_RING:
                    f = max(f for f in RUN0 if RUN0[f] <= r - FW_RING)
                    k = r - FW_RING - RUN0[f]
                    sp.wait_ge(score_full, SCORE[(("ffn", f), "D", k, G - 1)] + 1)
                sp.dma_start(w1[:, s, :], w1_all[r]).then_inc(fw_in[s], 16)
                sp.dma_start(w2[:, s, :], w2_all[r]).then_inc(fw_in[s], 16)

            for g in range(PATCH_RING):
                load_patch(g)
            load_aw(0)
            for g in range(PATCH_RING, G):
                load_patch(g)
            load_aw(1)
            for r in range(FW_RING):
                load_fw(r)
            for st in stages():
                if st[0] == "att" and st[1] + 2 < NATT:
                    load_aw(st[1] + 2)
                if st[0] == "ffn":
                    for k in range(len(ffn_runs(st[1]))):
                        if RUN0[st[1]] + k + FW_RING < NRUNS:
                            load_fw(RUN0[st[1]] + k + FW_RING)
            for g in range(G):
                n = min(TG, T_REAL - g * TG)
                sp.wait_ge(norm_done, READY[(None, g)] + 1)
                sp.dma_start(out[g * TG:g * TG + n, :], xn[0:n, g, :]).then_inc(out_done, 16)
            sp.wait_ge(out_done, 16 * G)

        @block.tensor
        def _(pe):
            def proj_bank(key):
                n = PROJ[key]
                if n >= 2:
                    pe.wait_ge(proj_taken[n % 2], n // 2)
                return ps_proj[:, n % 2, :]

            def proj_out(key):
                n = PROJ[key]
                pe.wait_ge(proj_taken[n % 2], n // 2 + 1)

            def score_bank(key):
                n = SCORE[key]
                if n >= 2:
                    pe.wait_ge(score_taken[n % 2], n // 2)
                return ps_score[:, n % 2, :]

            def turn(st, g):
                n = TURNED[(st, "A", g)]
                pe.wait_ge(norm_done, READY[(st, g)] + 1)
                if n:
                    pe.wait_ge(xt_ready, n)
                src = x if st == ("att", DIAG) else xn
                for c in range(2):
                    last = pe.transpose(ps_turn[0:KC, c * TG:(c + 1) * TG], src[:, g, c * KC:(c + 1) * KC], ident)
                if st == ("att", NEIGH):
                    for c in range(2):
                        last = pe.matmul(ps_turn[0:KC, (2 + c) * TG:(3 + c) * TG], src[:, g, c * KC:(c + 1) * KC],
                                         band, start=True, stop=True)
                last.then_inc(turn_full, 1)

            def att_step(st, step):
                a = st[1]
                s = ATTS[a]
                kind, g = step[0], step[1]
                par = g % 2
                key = (st, *step)
                if kind == "A":
                    turn(st, g)
                elif kind == "TOK":
                    bank = proj_bank(key)
                    pe.wait_ge(patch_in[g % PATCH_RING], 16 * (g // PATCH_RING + 1))
                    for c in range(PCH):
                        last = pe.matmul(bank[0:TG, 0:C], patch[:, g % PATCH_RING, c, :], tokw[:, c, :],
                                         start=(c == 0), stop=(c == PCH - 1))
                    last.then_inc(proj_full, 1)
                elif kind in ("Q", "K"):
                    j = step[2]
                    bank = proj_bank(key)
                    pe.wait_ge(xt_ready, TURNED[(st, "A", g)] + 1)
                    width = F if s.t5 else QK_SMALL
                    which = 0 if kind == "Q" else 1
                    if a == NEIGH:
                        parts = [(aw_part(a % 2, (2 * which + i) * 2 * width, width), i) for i in range(2)]
                    else:
                        parts = [(aw_part(a % 2, which * 2 * width, width), 0)]
                    for i in range(3):
                        m = 3 * j + i
                        terms = []
                        for w, banded in parts:
                            for c in range(2):
                                k = KC + 1 if a == NEIGH and c == 0 else KC
                                src = xband[0:k, par, c, :] if banded else xt[0:k, c, tokens(g)]
                                terms.append((w[0:k, c, m * 128:(m + 1) * 128], src))
                        for n, (w, src) in enumerate(terms):
                            last = pe.matmul(bank[:, i * TG:(i + 1) * TG], w, src, start=(n == 0),
                                             stop=(n == len(terms) - 1))
                    last.then_inc(proj_full, 1)
                elif kind == "V":
                    j = step[2]
                    bank = proj_bank(key)
                    width = F if s.t5 else C
                    at = (4 if s.t5 or a != NEIGH else 8) * (F if s.t5 else QK_SMALL)
                    w = aw_part(a % 2, at, width)
                    n = width // s.items
                    for c in range(2):
                        k = KC + 1 if a == NEIGH and c == 0 else KC
                        last = pe.matmul(bank[0:TG, 0:n], xt[0:k, c, tokens(g)], w[0:k, c, j * n:(j + 1) * n],
                                         start=(c == 0), stop=(c == 1))
                    last.then_inc(proj_full, 1)
                elif kind == "S":
                    u = step[2]
                    bank = score_bank(key)
                    if u == 0:
                        for what in ("Q", "K", "V"):
                            for j in range(s.items):
                                proj_out((st, what, g, j))
                    if s.pe_mask:
                        pe.matmul(bank[0:TG, 0:3 * TG], identb[:], maskb[:, a, :, :].rearrange("p h k -> p (h k)"),
                                  start=True, stop=False, skip_group_check=True)
                    for i, (c, p) in enumerate(s.heads(u)):
                        last = pe.matmul(bank[0:TG, i * TG:(i + 1) * TG], qt[p:p + s.rows, par, c, :],
                                         kt[p:p + s.rows, par, c, :], start=not s.pe_mask, stop=True,
                                         skip_group_check=True)
                    last.then_inc(score_full, 1)
                elif kind == "PT":
                    u = step[2]
                    n = unit(a, g, u)
                    pe.wait_ge(prob_ready, n + 1)
                    if n:
                        pe.wait_ge(pt_taken, n)
                    for i in range(3):
                        last = pe.transpose(ps_pt[0:TG, i * TG:(i + 1) * TG], prob[:, n % 3, i, :], ident)
                    last.then_inc(pt_full, 1)
                elif kind == "PV":
                    u = step[2]
                    pe.wait_ge(pt_taken, unit(a, g, u) + 1)
                    if u == 0 and a * G + g:
                        pe.wait_ge(o_ready, a * G + g)
                    v = v_of(a)
                    for i, (c, p) in enumerate(s.heads(u)):
                        h = s.head(c, p)
                        at = (h % 6) * (s.d + 1)
                        last = pe.matmul(ps_o[0:TG, h // 6, at:at + s.d + 1], probt[:, u % 2, i, :], v[:, (a * G + g) % 3, h, :],
                                         start=True, stop=True, skip_group_check=True)
                    if u == 3:
                        last.then_inc(o_full, 1)
                elif kind == "OT":
                    j = step[2]
                    bank = proj_bank(key)
                    pe.wait_ge(o_ready, a * G + g + 1)
                    n = s.ochunks // s.items
                    for i in range(n):
                        m = j * n + i
                        last = pe.transpose(bank[0:s.och, i * TG:(i + 1) * TG],
                                            o[:, par, m * s.och:(m + 1) * s.och], ident)
                    last.then_inc(proj_full, 1)
                elif kind == "Y":
                    bank = proj_bank(key)
                    for j in range(s.items):
                        proj_out((st, "OT", g, j))
                    if s.t5:
                        w = wo[:, a % 2, :].rearrange("p (c n) -> p c n", c=FC)
                    else:
                        w = aw_part(a % 2, 4 * QK_SMALL + 2 * C, C)
                    for c in range(s.ochunks):
                        last = pe.matmul(bank[0:TG, 0:C], ot[0:s.och, par, c, :], w[0:s.och, c, :],
                                         start=(c == 0), stop=(c == s.ochunks - 1))
                    last.then_inc(proj_full, 1)

            def ffn_step(st, step):
                f = st[1]
                kind = step[0]
                key = (st, *step)
                if kind == "A":
                    turn(st, step[1])
                elif kind == "L":
                    g = step[1]
                    bank = score_bank(key)
                    pe.wait_ge(xt_ready, TURNED[(st, "A", g)] + 1)
                    for c in range(2):
                        last = pe.matmul(bank[0:TG, 0:E], xt[0:KC, c, tokens(g)], gatew[:, c, WG[f], :],
                                         start=(c == 0), stop=(c == 1))
                    last.then_inc(score_full, 1)
                elif kind == "CNT":
                    bank = score_bank(key)
                    pe.wait_ge(hot_ready, 1)
                    rhs = both[:].rearrange("p g e -> p (g e)")
                    pe.matmul(bank[0:TG, 0:G * E], before_m, rhs, start=True, stop=True)
                    pe.matmul(bank[0:TG, G * E:2 * G * E], ones_m, rhs, start=True, stop=True).then_inc(score_full, 1)
                elif kind == "U":
                    _, k, b, m = step
                    r = RUN0[f] + k
                    slot = r % FW_RING
                    bank = proj_bank(key)
                    if m == 0 and b == 0:
                        pe.wait_ge(fw_in[slot], 32 * (r // FW_RING + 1))
                    g0, n = BLOCKS[b]
                    if m == 0 and k == 0:
                        pe.wait_ge(xt_ready, TURNED[(st, "A", g0 + n - 1)] + 1)
                    w = w1[:, slot, :].rearrange("p (c n) -> p c n", c=2)
                    for c in range(2):
                        last = pe.matmul(bank[:, 0:n * TG], w[:, c, m * 128:(m + 1) * 128], xt[0:KC, c, tokens(g0, n)],
                                         start=(c == 0), stop=(c == 1))
                    last.then_inc(proj_full, 1)
                elif kind == "D":
                    _, k, g = step
                    r = RUN0[f] + k
                    slot = r % FW_RING
                    bank = score_bank(key)
                    b = min(g // 4, 2)
                    if g == BLOCKS[b][0]:
                        for m in range(FC - 2, FC):
                            proj_out((st, "U", k, b, m))
                    at = (g - BLOCKS[b][0]) * TG
                    w = w2[:, slot, :].rearrange("p (c n) -> p c n", c=FC)
                    for m in range(FC):
                        last = pe.matmul(bank[0:TG, 0:C], hid[:, (3 * r + b) % 2, m, at:at + TG], w[:, m, :],
                                         start=(m == 0), stop=(m == FC - 1))
                    last.then_inc(score_full, 1)

            pe.wait_ge(const_in, 16 * NCONST)
            pe.wait_ge(setup_done, 1)
            for st in stages():
                if st[0] == "att":
                    a = st[1]
                    uses = sum(32 if b >= T5 else 16 for b in range(a % 2, a + 1, 2))
                    pe.wait_ge(aw_in[a % 2], uses)
                    if a < T5:
                        pe.wait_ge(aw_scaled, a + 1)
                for step in order(st):
                    (att_step if st[0] == "att" else ffn_step)(st, step)

        @block.scalar
        def _(act):
            def take_proj(key):
                n = PROJ[key]
                act.wait_ge(proj_full, n + 1)
                return ps_proj[:, n % 2, :], proj_taken[n % 2]

            def turned(st, g):
                n = TURNED[(st, "A", g)]
                act.wait_ge(turn_full, n + 1)
                if st in GAIN:
                    for c in range(2):
                        last = act.activation(xt[0:KC, c, tokens(g)], ps_turn[0:KC, c * TG:(c + 1) * TG], ACT.Copy,
                                              scale=gain[:, c, GAIN[st]:GAIN[st] + 1])
                else:
                    last = act.activation(xt[0:KC, :, tokens(g)],
                                          ps_turn[0:KC, 0:2 * TG].rearrange("p (c n) -> p c n", c=2), ACT.Copy)
                    if st == ("att", NEIGH):
                        last = act.activation(xband[0:KC, g % 2, :, :],
                                              ps_turn[0:KC, 2 * TG:4 * TG].rearrange("p (c n) -> p c n", c=2), ACT.Copy)
                last.then_inc(xt_ready, 1)

            act.wait_ge(const_in, 16 * NCONST)
            act.wait_ge(setup_done, 1)
            gates = 0
            for st in stages():
                for step in order(st):
                    kind = step[0]
                    key = (st, *step)
                    if kind == "A":
                        turned(st, step[1])
                    elif kind in ("Q", "K"):
                        bank, taken = take_proj(key)
                        j = step[2]
                        dst = qt if kind == "Q" else kt
                        act.activation(dst[:, step[1] % 2, 3 * j:3 * j + 3, :],
                                       bank[:, 0:3 * TG].rearrange("p (c n) -> p c n", c=3), ACT.Copy).then_inc(taken, 1)
                    elif kind == "E":
                        _, g, u = step
                        a = st[1]
                        n = SCORE[(st, "S", g, u)]
                        if ATTS[a].t5:
                            act.wait_ge(shifted, unit(a - T5, g, u) + 1)
                        else:
                            act.wait_ge(score_taken[n % 2], n // 2 + 1)
                        act.activation(prob[:, unit(a, g, u) % 3, :, :], prob[:, unit(a, g, u) % 3, :, :], ACT.Exp).then_inc(prob_ready, 1)
                    elif kind == "PT":
                        _, g, u = step
                        act.wait_ge(pt_full, unit(st[1], g, u) + 1)
                        act.activation(probt[:, u % 2, :, :], ps_pt[0:TG, 0:3 * TG].rearrange("p (c n) -> p c n", c=3),
                                       ACT.Copy).then_inc(pt_taken, 1)
                    elif kind == "OT":
                        bank, taken = take_proj(key)
                        _, g, j = step
                        s = ATTS[st[1]]
                        n = s.ochunks // s.items
                        act.activation(ot[0:s.och, g % 2, j * n:(j + 1) * n, :],
                                       bank[0:s.och, 0:n * TG].rearrange("p (c n) -> p c n", c=n),
                                       ACT.Copy).then_inc(taken, 1)
                    elif kind == "GATE":
                        gates += 1
                        act.wait_ge(gap_ready, gates)
                        act.activation(egap[:], gap[:], ACT.Exp).then_inc(egap_ready, 1)
                    elif kind == "U":
                        bank, taken = take_proj(key)
                        _, k, b, m = step
                        r = RUN0[st[1]] + k
                        n = BLOCKS[b][1] * TG
                        func = ACT.Relu if ffn_runs(st[1])[k] < 0 else ACT.Gelu
                        act.activation(hid[:, (3 * r + b) % 2, m, 0:n], bank[:, 0:n], func).then_inc(taken, 1)

        @block.gpsimd
        def _(pool):
            steps = [0]

            def link(ins):
                steps[0] += 1
                ins.then_inc(pool_step, 1)
                pool.wait_ge(pool_step, steps[0])

            pool.wait_ge(const_in, 16 * NCONST)
            pool.wait_ge(setup_done, 1)
            for (st, kind, g), n in NORMS.items():
                m = n % NORM_RING
                v, r, t = var[:, m:m + 1], rs[:, m:m + 1], tmp[:, 0:1]
                pool.wait_ge(stats_ready, n + 1)
                for _ in range(3):
                    link(pool.tensor_tensor(t, r, r, ALU.mult))
                    link(pool.tensor_tensor(t, t, v, ALU.mult))
                    link(pool.tensor_scalar(t, t, -0.5, 1.5, ALU.mult, ALU.add))
                    link(pool.tensor_tensor(r, r, t, ALU.mult))
                mean, xg, xng = mv[:, m, 0:1], x[:, g, :], xn[:, g, :]

                def centred(dst, src):
                    return pool.tensor_scalar(dst, src, mean, r, ALU.subtract, ALU.mult)

                def scaled(dst, src):
                    return pool.tensor_scalar(dst, src, r, None, ALU.mult)

                if kind == "TOK":
                    link(centred(xng, xg))
                    link(pool.tensor_tensor(xng, xng, row[:, R_LNG, :], ALU.mult))
                    last = pool.tensor_tensor(xng, xng, row[:, R_LNB, :], ALU.add)
                elif kind == "N2":
                    if st == ("att", NEIGH):
                        last = centred(xng, xg)
                    elif st == ("att", DIAG):
                        last = scaled(xng, xg)
                    else:
                        last = centred(xng, held[:, g, :])
                elif st in (("att", NEIGH), ("att", DIAG)):
                    link(centred(xg, wide[:, m, :]))
                    last = pool.tensor_copy(held[:, g, :], xg)
                elif st == ("ffn", 0):
                    last = centred(xg, wide[:, m, :])
                elif st == ("att", CAUSAL):
                    last = centred(xng, xg)
                elif st == ("ffn", LAYERS):
                    link(scaled(xng, xg))
                    link(pool.tensor_tensor(xng, xng, row[:, R_LNF, :], ALU.mult))
                    last = pool.tensor_tensor(held[:, g, :], held[:, g, :], xng, ALU.add)
                else:
                    last = scaled(xng, xg)
                last.then_inc(norm_done, 1)

        @block.vector
        def _(dve):
            steps = [0]

            def link(ins):
                steps[0] += 1
                ins.then_inc(dve_step, 1)
                dve.wait_ge(dve_step, steps[0])

            def tell(ins, which, value):
                ins.then_inc(which, 1)
                dve.wait_ge(which, value)

            def start_norm(key, src, rms, eps):
                n = NORMS[key]
                m = n % NORM_RING
                if rms is None:
                    rms = False
                link(dve.bn_stats(stat[:], src))
                link(dve.bn_aggr(mv[:, m, :], stat[:]))
                v, r = var[:, m:m + 1], rs[:, m:m + 1]
                if rms:
                    link(dve.scalar_tensor_tensor(out=mv[:, m, 1:2], in0=mv[:, m, 0:1], scalar=mv[:, m, 0:1],
                                                  in1=mv[:, m, 1:2], op0=ALU.mult, op1=ALU.add))
                link(dve.tensor_scalar(v, mv[:, m, 1:2], eps, None, ALU.add))
                tell(dve.tensor_scalar(r.bitcast(I32), v.bitcast(I32), -0.5, RSQRT_SEED, ALU.mult, ALU.add),
                     stats_ready, n + 1)

            def norm_slot(key):
                n = NORMS[key]
                if n >= NORM_RING:
                    dve.wait_ge(norm_done, n - NORM_RING + 1)
                return n % NORM_RING

            def take_proj(key):
                n = PROJ[key]
                dve.wait_ge(proj_full, n + 1)
                return ps_proj[:, n % 2, :], proj_taken[n % 2], n // 2 + 1

            def take_score(key):
                n = SCORE[key]
                dve.wait_ge(score_full, n + 1)
                return ps_score[:, n % 2, :], score_taken[n % 2], n // 2 + 1

            def softmax_shift(st, step, t5_units):
                a, (_, g, u) = st[1], step
                bank, taken, value = take_score((st, *step))
                scores = bank[0:TG, 0:3 * TG].rearrange("p (h k) -> p h k", h=3)
                dst = prob[:, unit(a, g, u) % 3, :, :]
                if ATTS[a].t5:
                    tell(dve.tensor_tensor(dst, scores, relbias[:, 3 * u:3 * u + 3, :], ALU.add), taken, value)
                    scores = dst
                link(dve.tensor_reduce(negmax[:], scores, AX.X, ALU.max, negate=True))
                ins = dve.tensor_tensor(dst, scores, negmax[:].unsqueeze(2).to_broadcast([TG, 3, TG]), ALU.add)
                if ATTS[a].t5:
                    tell(ins, shifted, unit(a - T5, g, u) + 1)
                else:
                    tell(ins, taken, value)

            def divide(a, g):
                s = ATTS[a]
                dve.wait_ge(o_full, a * G + g + 1)
                n = 6 * (s.d + 1)
                view = ps_o[0:TG, :, 0:n].rearrange("p b (h d) -> p b h d", h=6)
                link(dve.reciprocal(rden[:].rearrange("p (b h) -> p b h", b=2), view[:, :, :, s.d]))
                for b in range(2):
                    ins = dve.tensor_tensor(
                        o[:, g % 2, b * 6 * s.d:(b + 1) * 6 * s.d].rearrange("p (h d) -> p h d", h=6),
                        view[:, b, :, 0:s.d],
                        rden[:, 6 * b:6 * b + 6].unsqueeze(2).to_broadcast([TG, 6, s.d]), ALU.mult)
                    if b == 0:
                        link(ins)
                tell(ins, o_ready, a * G + g + 1)

            dve.wait_ge(const_in, 16 * NCONST)
            link(dve.tensor_copy(identb[:], ident))
            for a, at in enumerate((K_BLOCK, K_CAUSAL, K_DIAG)):
                for i in range(3):
                    link(dve.tensor_copy(maskb[:, a, i, :], const[:, at:at + TG]))
            link(dve.tensor_tensor(relbias[:], relbias[:],
                                   const[:, K_BLOCK:K_BLOCK + TG].unsqueeze(1).to_broadcast([TG, H, TG]), ALU.add))
            link(dve.memset(v64[:], 1.0))
            link(dve.memset(v16[:], 1.0))
            link(dve.memset(xt[KC:KC + 1, 0, :], 1.0))
            link(dve.tensor_tensor(row[:, R_POS, :], row[:, R_POS, :], row[:, R_TOKB, :], ALU.add))
            tell(dve.memset(rden[:], 0.0), setup_done, 1)

            def scale_weights(a):
                dve.wait_ge(aw_in[a % 2], 16 * (a // 2 + 1))
                n = 2 * QK_SMALL
                k = KC + 1 if a == NEIGH else KC
                if a == NEIGH:
                    s = float(SMALL_D) ** -0.5
                    link(dve.tensor_scalar(aw[0:k, 0, 0:n], aw[0:k, 0, 0:n], 1.2 * s, None, ALU.mult))
                    ins = dve.tensor_scalar(aw[0:k, 0, n:2 * n], aw[0:k, 0, n:2 * n], -0.2 * s, None, ALU.mult)
                elif a == CAUSAL:
                    ins = dve.tensor_scalar(aw[0:k, 1, 0:n], aw[0:k, 1, 0:n], float(SMALL_D) ** -0.5, None, ALU.mult)
                else:
                    w = aw_part(0, 0, QK_SMALL)[0:k]
                    ins = dve.tensor_tensor(w, w, hscale[:].unsqueeze(1).to_broadcast([k, 2, QK_SMALL]), ALU.mult)
                tell(ins, aw_scaled, a + 1)

            gates = 0
            for st in stages():
                if st[0] == "att" and st[1] < T5:
                    scale_weights(st[1])
                for step in order(st):
                    kind = step[0]
                    key = (st, *step)
                    if kind == "TOK":
                        g = step[1]
                        bank, taken, value = take_proj(key)
                        tell(dve.tensor_tensor(x[:, g, :], bank[0:TG, 0:C], row[:, R_POS, :], ALU.add), taken, value)
                        norm_slot((st, "TOK", g))
                        start_norm((st, "TOK", g), x[:, g, :], False, LN_EPS)
                    elif kind == "V":
                        _, g, j = step
                        bank, taken, value = take_proj(key)
                        s = ATTS[st[1]]
                        hs = H // s.items
                        tell(dve.tensor_copy(v_of(st[1])[:, (st[1] * G + g) % 3, j * hs:(j + 1) * hs, 0:s.d],
                                             bank[0:TG, 0:hs * s.d].rearrange("p (h d) -> p h d", h=hs)), taken, value)
                    elif kind == "S":
                        softmax_shift(st, step, 0)
                    elif kind == "PV" and step[2] == 3:
                        g = step[1]
                        divide(st[1], g)
                        if st[1] == NEIGH:
                            m = norm_slot((st, "PV", g))
                            link(dve.tensor_tensor(wide[:, m, :], o[:, g % 2, 0:C], x[:, g, :], ALU.add))
                            start_norm((st, "PV", g), wide[:, m, :], False, LN_EPS)
                    elif kind == "Y":
                        g, a = step[1], st[1]
                        bank, taken, value = take_proj(key)
                        y = bank[0:TG, 0:C]
                        m = norm_slot((st, "Y", g))
                        if a == DIAG:
                            tell(dve.scalar_tensor_tensor(out=wide[:, m, :], in0=x[:, g, :], scalar=2.0, in1=y,
                                                          op0=ALU.mult, op1=ALU.add), taken, value)
                            link(dve.tensor_tensor(wide[:, m, :], wide[:, m, :], row[:, R_BPROJ, :], ALU.add))
                            start_norm((st, "Y", g), wide[:, m, :], False, LN_EPS)
                        else:
                            tell(dve.tensor_tensor(x[:, g, :], y, x[:, g, :], ALU.add), taken, value)
                            start_norm((st, "Y", g), x[:, g, :], a >= T5, RMS_EPS if a >= T5 else LN_EPS)
                    elif kind == "N2":
                        g = step[1]
                        before = "PV" if st == ("att", NEIGH) else "Y" if st[0] == "att" else "D"
                        dve.wait_ge(norm_done, NORMS[(st, before, g)] + 1)
                        norm_slot((st, "N2", g))
                        rms = st == ("att", DIAG)
                        src = held[:, g, :] if st[0] == "ffn" else x[:, g, :]
                        start_norm((st, "N2", g), src, rms, RMS_EPS if rms else LN_EPS)
                    elif kind == "L":
                        g = step[1]
                        bank, taken, value = take_score(key)
                        tell(dve.tensor_copy(logit[:, g, :], bank[0:TG, 0:E]), taken, value)
                        link(dve.max(best[:, g, :], logit[:, g, :]))
                        link(dve.max_index(best_at[:, g, :], best[:, g, :], logit[:, g, :]))
                        if g == G - 1:
                            link(dve.tensor_copy(atf[:], best_at[:, :, 0:2]))
                            for k, hot in enumerate((hot1, hot2)):
                                link(dve.tensor_tensor(hot[:], iota, atf[:, :, k:k + 1].to_broadcast([TG, G, E]),
                                                       ALU.is_equal))
                            if st[1] == 0:
                                tell(dve.tensor_tensor(both[:], hot1[:], hot2[:], ALU.add), hot_ready, 1)
                    elif kind == "CNT":
                        bank, taken, value = take_score(key)
                        tell(dve.tensor_copy(cnt[:].rearrange("p a g e -> p (a g e)"), bank[0:TG, 0:2 * G * E]),
                             taken, value)
                        for g in range(1, G - 1):
                            link(dve.tensor_tensor(cnt[:, 1, g, :], cnt[:, 1, g, :], cnt[:, 1, g - 1, :], ALU.add))
                        link(dve.tensor_tensor(cnt[:, 0, 1:G, :], cnt[:, 0, 1:G, :], cnt[:, 1, 0:G - 1, :], ALU.add))
                    elif kind == "GATE":
                        gates += 1
                        tell(dve.tensor_tensor(gap[:], best[:, :, 1], best[:, :, 0], ALU.subtract), gap_ready, gates)
                        dve.wait_ge(egap_ready, gates)
                        link(dve.tensor_scalar(p1[:], egap[:], 1.0, None, ALU.add))
                        link(dve.reciprocal(p1[:], p1[:]))
                        link(dve.tensor_tensor(p2[:], p1[:], egap[:], ALU.mult))
                        link(dve.tensor_tensor(hot1[:], hot1[:], p1[:].unsqueeze(2).to_broadcast([TG, G, E]), ALU.mult))
                        link(dve.tensor_tensor(hot2[:], hot2[:], p2[:].unsqueeze(2).to_broadcast([TG, G, E]), ALU.mult))
                        link(dve.tensor_tensor(cw[:], hot1[:], hot2[:], ALU.add))
                        if st[1] == 0:
                            link(dve.scalar_tensor_tensor(
                                out=cw[:].rearrange("p g e -> p (g e)"),
                                in0=cnt[:, 0, :, :].rearrange("p g e -> p (g e)"), scalar=float(CAP),
                                in1=cw[:].rearrange("p g e -> p (g e)"), op0=ALU.is_lt, op1=ALU.mult))
                    elif kind == "D":
                        _, k, g = step
                        f = st[1]
                        runs = ffn_runs(f)
                        bank, taken, value = take_score(key)
                        e = runs[k]
                        if e < 0:
                            ins = dve.tensor_tensor(x[:, g, :], bank[0:TG, 0:C], x[:, g, :], ALU.add)
                        else:
                            ins = dve.scalar_tensor_tensor(out=x[:, g, :], in0=bank[0:TG, 0:C],
                                                           scalar=cw[:, g, e:e + 1], in1=x[:, g, :], op0=ALU.mult,
                                                           op1=ALU.add)
                        tell(ins, taken, value)
                        if k == len(runs) - 1:
                            m = norm_slot((st, "D", g))
                            if f == 0:
                                link(dve.tensor_tensor(wide[:, m, :], held[:, g, :], x[:, g, :], ALU.add))
                                start_norm((st, "D", g), wide[:, m, :], False, LN_EPS)
                            else:
                                start_norm((st, "D", g), x[:, g, :], True, RMS_EPS)


def lay_out(inp):
    f = {k: np.asarray(v) for k, v in inp.items()}
    x = f["x"]
    z = np.zeros((G * IPG, NTOK, PD), np.float32)
    p = x.reshape(B, CIN, GRID, PATCH, GRID, PATCH).transpose(0, 2, 4, 1, 3, 5).reshape(B, GRID * GRID, PD)
    z[:B, 1:] = p
    patches = z.reshape(G, TG, PCH, 128).transpose(0, 3, 2, 1)

    def chunks(w, k):
        return w.reshape(-1, k, w.shape[-1]).transpose(1, 0, 2)

    def flat(w):
        return w.reshape(w.shape[0], -1)

    t = np.arange(TG)
    same = (t[:, None] // NTOK) == (t[None, :] // NTOK)
    const = np.zeros((TG, K_WIDTH), np.float32)
    const[:, K_IDENT:K_IDENT + TG] = np.eye(TG)
    const[:, K_BAND:K_BAND + TG] = same & (abs(t[:, None] - t[None, :]) <= 1)
    const[:, K_BLOCK:K_BLOCK + TG] = np.where(same, 0.0, NEG)
    const[:, K_CAUSAL:K_CAUSAL + TG] = np.where(same & (t[:, None] >= t[None, :]), 0.0, NEG)
    const[:, K_DIAG:K_DIAG + TG] = np.where(same & (t[:, None] != t[None, :]), 0.0, NEG)
    const[:, K_BEFORE:K_BEFORE + TG] = t[:, None] < t[None, :]
    const[:, K_ONES:K_ONES + TG] = 1.0
    const[:, K_IOTA:] = np.tile(np.arange(E), G)
    edge = np.where((t % NTOK == 0) | (t % NTOK == NTOK - 1), 2.0, 3.0).astype(np.float32)[None]

    rows = np.zeros((TG, 6, C), np.float32)
    rows[:, R_LNG] = f["L0_attn_ln_g"]
    rows[:, R_LNB] = f["L0_attn_ln_b"]
    rows[:, R_BPROJ] = f["L1_attn_b_proj"]
    rows[:, R_LNF] = f["L1_ffn_ln_f"]
    pos = f["L0_tok_positions"]
    ih = np.arange(GRID) * pos.shape[2] // GRID
    pos = pos[0][:, ih][:, :, ih].reshape(C, GRID * GRID).T
    for i in range(IPG):
        rows[i * NTOK, R_POS] = f["L0_tok_cls_embedding"][0, 0]
        rows[i * NTOK + 1:(i + 1) * NTOK, R_POS] = pos
        rows[i * NTOK + 1:(i + 1) * NTOK, R_TOKB] = f["L0_tok_b"]

    gains = np.zeros((NGAIN, C), np.float32)
    gains[0], gains[1] = f["L0_ffn_ln1_w"], f["L0_ffn_ln2_w"]
    gains[2::2], gains[3::2] = f["L1_ffn_ln1"], f["L1_ffn_ln2"]
    gains = gains.reshape(NGAIN, 2, KC).transpose(2, 1, 0)
    gw = np.stack([f["L0_ffn_w_g"].T, f["L1_ffn_gate_w"][0], f["L1_ffn_gate_w"][1]])
    gw = gw.reshape(3, 2, KC, E).transpose(2, 1, 0, 3)
    hs = np.broadcast_to(np.repeat(f["L1_attn_scale"], 32)[None], (KC, QK_SMALL))

    rel = np.arange(NTOK)[None, :] - np.arange(NTOK)[:, None]
    nb, maxd = f["L1_ffn_rel_emb"].shape[0] // 2, 128
    n = np.abs(rel)
    me = nb // 2
    nf = np.maximum(n, 1).astype(np.float32)
    large = me + (np.log(nf / np.float32(me)) / np.float32(np.log(maxd / me)) * np.float32(nb - me)).astype(np.int32)
    buckets = (rel > 0) * nb + np.where(n < me, n, np.minimum(large, nb - 1))
    heads = [ATTS[T5].head(c, s) for u in range(4) for c, s in ATTS[T5].heads(u)]
    bias = np.zeros((TG, H, TG), np.float32)
    for i in range(IPG):
        sl = slice(i * NTOK, (i + 1) * NTOK)
        bias[sl, :, sl] = f["L1_ffn_rel_emb"][buckets].transpose(0, 2, 1)[:, heads]

    def spread(w, at):
        out = np.zeros((w.shape[0], H, 32), np.float32)
        out[:, :, at:at + SMALL_D] = w.reshape(-1, H, SMALL_D)
        return out.reshape(-1, QK_SMALL)

    def with_bias(w, b):
        out = np.zeros((KC + 1, 2, w.shape[1]), np.float32)
        out[:KC] = chunks(w, KC)
        out[KC, 0] = b
        return flat(out)

    w, b = f["L0_attn_qkv_w"].T, f["L0_attn_qkv_b"][None]
    aw_neigh = np.concatenate(
        [with_bias(spread(w[:, i * C:(i + 1) * C], at), spread(b[:, i * C:(i + 1) * C], at)[0])
         for i in range(2) for at in (0, SMALL_D)] + [with_bias(w[:, 2 * C:], b[0, 2 * C:])], 1)

    def small(w, wo):
        w = w.T
        return np.concatenate([flat(chunks(spread(w[:, i * C:(i + 1) * C], 0), KC)) for i in range(2)]
                              + [flat(chunks(w[:, 2 * C:], KC)), flat(chunks(wo.T, KC))], 1)

    aw_causal = small(f["L0_ffn_c_attn_w"], f["L0_ffn_c_proj_w"])
    aw_diag = small(f["L1_attn_w_qkv"], f["L1_attn_w_proj"])
    aw_t5 = np.stack([np.concatenate([flat(chunks(f[f"L1_ffn_attn_{n}"][l], KC)) for n in "qkv"], 1)
                      for l in range(LAYERS)])
    wo_t5 = np.stack([flat(chunks(f["L1_ffn_attn_o"][l], 128)) for l in range(LAYERS)])
    up, down = list(f["L0_ffn_c_fc"]), list(f["L0_ffn_c_proj_e"])
    for l in range(LAYERS):
        up.append(f["L1_ffn_ffn_wi"][l])
        down.append(f["L1_ffn_ffn_wo"][l])
        if l in MOE_LAYERS:
            up += list(f["L1_ffn_moe_w1"][MOE_LAYERS.index(l)])
            down += list(f["L1_ffn_moe_w2"][MOE_LAYERS.index(l)])
    w1 = np.stack([flat(chunks(w, KC)) for w in up])
    w2 = np.stack([flat(chunks(w, 128)) for w in down])
    out = [patches, chunks(f["L0_tok_W"], 128), const, rows, gains, gw, hs, bias, edge,
           aw_neigh, aw_causal, aw_diag, aw_t5, wo_t5, w1, w2]
    return [np.ascontiguousarray(a, dtype=np.float32) for a in out]


def kernel(**inputs):
    import concourse.bacc as bacc
    from concourse.bass_utils import run_bass_kernel_spmd

    nc = bacc.Bacc("TRN2", target_bir_lowering=False, num_devices=1)
    names = ["patches", "tok_w", "consts", "rows", "gains", "gates_w", "head_scale", "bias_src", "edge", "aw_neigh",
             "aw_causal", "aw_diag", "aw_t5", "wo_t5", "w1_all", "w2_all"]
    arrays = {n + "_dram": a for n, a in zip(names, lay_out(inputs))}
    args = [nc.dram_tensor(n, a.shape, F32, kind="ExternalInput").ap() for n, a in arrays.items()]
    out = nc.dram_tensor("out_dram", (T_REAL, C), F32, kind="ExternalOutput").ap()
    tower(nc, *args, out)
    r = run_bass_kernel_spmd(nc, [arrays], core_ids=[0])
    return r.results[0]["out_dram"].reshape(B, NTOK, C)
```

```python
from contextlib import ExitStack

import numpy as np

import concourse.bass as bass
from concourse import mybir

ALU = mybir.AluOpType
ACT = mybir.ActivationFunctionType
AX = mybir.AxisListType
F32 = mybir.dt.float32
F32R = mybir.dt.float32r
BF16 = mybir.dt.bfloat16
I32 = mybir.dt.int32
U32 = mybir.dt.uint32

B, CIN, IMGSZ, PATCH = 32, 3, 96, 16
GRID = IMGSZ // PATCH
NTOK = GRID * GRID + 1
C = 192
KC = C // 2
H = 12
IPG = 3
TG = IPG * NTOK
G = -(-B // IPG)
T = G * TG
T_REAL = B * NTOK
PD = CIN * PATCH * PATCH
PCH = PD // 128
F = 768
FC = F // 128
E = 8
TOP_K = 2
CAP = TOP_K * T_REAL // E
CAP += CAP % 2
LAYERS = 4
MOE_LAYERS = (1, 3)
NEG = -1.0e30
LN_EPS, RMS_EPS = 1e-5, 1e-6
SMALL_D = C // H
T5_D = 64
BLOCKS = [(0, 3), (3, 3), (6, 3), (9, 2)]
NB = len(BLOCKS)
BLOCK_OF = [b for b, (g0, n) in enumerate(BLOCKS) for _ in range(n)]
TP = TG + TG % 2
CX = 2 * 128
RSQRT_SEED = 1597463007.0

NEIGH, CAUSAL, DIAG, T5 = 0, 1, 2, 3
NATT = 3 + LAYERS


class Att:

    def __init__(self, a):
        self.a = a
        self.t5 = a >= T5
        self.d = T5_D if self.t5 else SMALL_D
        self.rows = 64 if self.t5 else 32
        self.per_chunk = 128 // self.rows
        self.chunks = H // self.per_chunk
        self.items = self.chunks // 3
        self.proj = a != NEIGH
        self.pe_mask = not self.t5
        self.och = 128 if self.t5 else KC
        self.ochunks = H * self.d // self.och

    def heads(self, u):
        if self.t5:
            return [(3 * (u // 2) + c, 64 * (u % 2)) for c in range(3)]
        return [(c, 32 * u) for c in range(3)]

    def head(self, chunk, start):
        return chunk * self.per_chunk + start // self.rows


ATTS = [Att(a) for a in range(NATT)]


def stages():
    out = [("att", 0), ("att", 1), ("ffn", 0), ("att", 2)]
    for l in range(LAYERS):
        out += [("att", T5 + l), ("ffn", 1 + l)]
    return out


def ffn_runs(f):
    if f == 0:
        return list(range(E))
    return [-1] + (list(range(E)) if f - 1 in MOE_LAYERS else [])


def is_moe(f):
    return f == 0 or f - 1 in MOE_LAYERS


RUN0 = {0: 0}
for _f in range(LAYERS):
    RUN0[_f + 1] = RUN0[_f] + len(ffn_runs(_f))
NRUNS = RUN0[LAYERS] + len(ffn_runs(LAYERS))
FFN_AFTER = {CAUSAL: 0} | {T5 + l: 1 + l for l in range(LAYERS)}


def qkv(a, g):
    return [(kind, g, j) for kind in ("Q", "K", "V") for j in range(ATTS[a].items)]


def att_order(a, last_stage, follower):
    s = ATTS[a]
    ffn_next = follower[0] == "ffn"
    out = []
    if a == NEIGH:
        out += [("SC", NEIGH), ("TOK", 0), ("TOK", 1), ("A", 0)] + qkv(a, 0) + [("TOK", 2), ("A", 1)]
    elif last_stage[0] == "ffn":
        out += qkv(a, 0)
    units = 4 * G
    fill, given = [], 0
    for n in range(units + 3):
        g, u = divmod(n, 4)
        if u == 0:
            fill = []
            if s.proj and 2 <= g:
                fill += [("OT", g - 2, j) for j in range(s.items)]
            if a == NEIGH and g + 3 < G:
                fill.append(("TOK", g + 3))
            more = qkv(a, g + 1) if g + 1 < G else []
            fill += more[:len(more) // 2]
            if s.proj and 2 <= g:
                fill.append(("Y", g - 2))
            fill += more[len(more) // 2:]
            if a in (NEIGH, DIAG) and g >= 3:
                fill.append(("N2", g - 3))
            if g + 2 < G:
                fill.append(("A", g + 2))
            if ffn_next and 3 <= g < G:
                fill.append(("next", ("A", g - 3)))
                if follower[1] == 0 and g >= 4:
                    fill.append(("next", ("L", g - 4)))
            if not ffn_next and g == G - 1:
                fill += [("next", ("A", 0)), ("next", ("A", 1))]
            if not ffn_next and g == G:
                fill += [("next", x) for x in qkv(follower[1], 0)]
            count, given, gap = len(fill), 0, 0
        if n == 8 and a == NEIGH:
            out.append(("SC", CAUSAL))
        if n == 1 and a in FFN_AFTER:
            out.append(("W", RUN0[FFN_AFTER[a]]))
        steps = []
        if n < units:
            steps.append(("S", g, u))
        if 1 <= n <= units:
            steps.append(("E", (n - 1) // 4, (n - 1) % 4))
        if 2 <= n < units + 2:
            steps.append(("PT", (n - 2) // 4, (n - 2) % 4))
        if 3 <= n:
            steps.append(("PV", (n - 3) // 4, (n - 3) % 4))
        for x in steps:
            out.append(x)
            if x[0] == "E":
                continue
            gap += 1
            upto = min(-(-count * gap // 12), count)
            out += fill[given:upto]
            given = max(given, upto)
        if u == 3:
            out += fill[given:]
            given = count
    out += fill[given:]
    if s.proj:
        out += [("OT", G - 1, j) for j in range(s.items)] + [("Y", G - 1)]
    if a in (NEIGH, DIAG):
        out += [("N2", g) for g in range(G) if ("N2", g) not in out]
    return out


def ffn_order(f, last):
    out = []
    runs = ffn_runs(f)
    before = []
    turns = [("A", g) for g in range(G - 3, G)]
    gates = [("L", g) for g in range(G - 4 if f == 0 else 0, G)] if is_moe(f) else []
    for k in range(len(runs)):
        for b, (g0, n) in enumerate(BLOCKS):
            for m in range(FC):
                out.append(("U", k, b, m))
                if turns and m != 1:
                    out.append(turns.pop(0))
                if gates and (b > 0 or m > 1):
                    out.append(gates.pop(0))
                if m % 2 and before and not (f == 0 and (k, b) == (0, 1)):
                    out.append(before.pop(0))
                if f == 0 and (k, b) == (0, 1):
                    out += {0: [("CNT",)], 1: [("SC", DIAG)], 2: [("GATE",)], 4: before}.get(m, [])
                    if m == 4:
                        before = []
                if m == 0 and b == 1 and k + 1 < len(runs) and not (f == 0 and k == 0):
                    out.append(("W", RUN0[f] + k + 1))
                if (f, k, b, m) == (0, 0, 1, 3):
                    out.append(("W", RUN0[f] + 1))
                if not last and k == len(runs) - 1 and b == NB - 1 and m in (2, 4):
                    out.append(("next", ("A", m // 2 - 1)))
            out += before
            before = [("D", k, g) for g in range(g0, g0 + n)]
            if f and is_moe(f) and (k, b) == (0, NB - 1):
                out += [("GATE",)]
    out += before
    if last:
        for g in range(G):
            at = out.index(("D", len(runs) - 1, min(g + 2, G - 1))) + 1
            out.insert(at if g + 2 < G else len(out), ("FIN", g))
    return out


def program():
    every = stages()
    out = []
    for i, st in enumerate(every):
        follower = every[i + 1] if i + 1 < len(every) else None
        steps = att_order(st[1], every[i - 1], follower) if st[0] == "att" else ffn_order(st[1], follower is None)
        for x in steps:
            out.append((follower, x[1]) if x[0] == "next" else (st, x))
    return out


PROGRAM = program()


def numbered():
    proj, score, turned, ready, norms, hidden = {}, {}, {}, {}, {}, {}
    every = stages()
    after = dict(zip(every, every[1:] + [None]))
    for st, step in PROGRAM:
        key = (st, *step)
        if step[0] in ("TOK", "Q", "K", "V", "OT", "Y", "U"):
            proj[key] = len(proj)
            if step[0] == "U":
                hidden[key] = len(hidden)
        elif step[0] in ("S", "L", "CNT", "D"):
            score[key] = len(score)
        elif step[0] == "A":
            turned[key] = len(turned)
        if step[0] in ("TOK", "Y", "N2") or (st == ("att", NEIGH) and step[0] == "PV" and step[2] == 3) \
                or (step[0] == "D" and step[1] == len(ffn_runs(st[1])) - 1):
            g = step[2] if step[0] == "D" else step[1]
            norms[(st, step[0], g)] = len(norms)
            ready[(st if step[0] == "TOK" else after[st], g)] = len(norms) - 1
    return proj, score, turned, ready, norms, hidden


PROJ, SCORE, TURNED, READY, NORMS, HIDDEN = numbered()
NORM_RING = 6
FW_RING = 2
PATCH_RING = 2

K_IDENT, K_BAND, K_BLOCK, K_CAUSAL, K_DIAG, K_BEFORE, K_ONES, K_IOTA = [TG * i for i in range(8)]
K_WIDTH = 7 * TG + G * E
R_LNG, R_LNB, R_BPROJ, R_LNF, R_POS, R_TOKB = range(6)
GAIN = {("att", 1): 0, ("ffn", 0): 1}
for _l in range(LAYERS):
    GAIN[("att", T5 + _l)] = 2 + 2 * _l
    GAIN[("ffn", 1 + _l)] = 3 + 2 * _l
NGAIN = 2 + 2 * LAYERS
WG = {0: 0, 2: 1, 4: 2}
QK_SMALL = 4 * 32 * 3
AWB_W = 4 * 2 * QK_SMALL + 2 * C
AWC_W = 2 * 2 * QK_SMALL + 2 * C + 2 * C
AWE_W = 3 * 2 * F
WO_W = FC * C


def tower(nc, patches, tok_w, consts, rows, gains, gains_ffn, gates_w, head_scale, bias_src, edge,
          aw_neigh, aw_causal, aw_diag, aw_t5, wo_t5, w1_all, w2_all, out):
    with ExitStack() as ctx:
        def sb(name, shape, dt=F32):
            return ctx.enter_context(nc.sbuf_tensor(name, shape, dt))

        def ps(name, shape):
            return ctx.enter_context(nc.psum_tensor(name, shape, F32))

        def sem(name):
            return ctx.enter_context(nc.semaphore(name))

        x = sb("x", [TG, G, C])
        held = sb("held", [TG, G, C])
        xn = sb("xn", [TG, G, CX])
        xt = sb("xt", [KC + 1, 2, 2, TG])
        xa_hi = sb("xa_hi", [128, G, TP], F32R)
        xa_lo = sb("xa_lo", [128, G, TP], F32R)
        xb = sb("xb", [128, G, TP], F32R)
        xband = sb("xband", [KC + 1, 2, 2, TG])
        patch = sb("patch", [128, PATCH_RING, PCH, TG])
        tokw = sb("tokw", [128, PCH, C])
        const = sb("const", [TG, K_WIDTH])
        row = sb("row", [TG, 6, C])
        gain = sb("gain", [KC, 2, NGAIN])
        gainf = sb("gainf", [128, 2, 1 + LAYERS])
        gatew = sb("gatew", [128, 2, 3, E])
        gate_hi = sb("gate_hi", [128, 2, 3, E], F32R)
        gate_lo = sb("gate_lo", [128, 2, 3, E], F32R)
        hscale = sb("hscale", [KC, QK_SMALL])
        identb = sb("identb", [TG, TG], BF16)
        maskb = sb("maskb", [TG, 3, 3, TG], BF16)
        relbias = sb("relbias", [TG, H, TG])
        aw_small = sb("aw_small", [KC + 1, AWB_W])
        aw_big = sb("aw_big", [KC, AWE_W])
        wo = sb("wo", [128, WO_W])
        w1_in = sb("w1_in", [128, 2, F])
        w2_in = sb("w2_in", [128, FC * C])
        w1_hi = sb("w1_hi", [128, FW_RING, 2, F], F32R)
        w1_lo = sb("w1_lo", [128, FW_RING, 2, F], F32R)
        w2_hi = sb("w2_hi", [128, FW_RING, FC, C], F32R)
        w2_lo = sb("w2_lo", [128, FW_RING, FC, C], F32R)
        v16 = sb("v16", [TG, 3, H, SMALL_D + 1])
        negmax = sb("negmax", [TG, 3])
        rden = sb("rden", [TG, H])
        stat = sb("stat", [TG, 6])
        mv = sb("mv", [TG, NORM_RING, 2])
        var = sb("var", [TG, NORM_RING])
        rs = sb("rs", [TG, NORM_RING])
        last_mv = sb("last_mv", [TG, 2])
        last_nr = sb("last_nr", [TG, 3])
        tmp = sb("tmp", [TG, 2])
        wide = sb("wide", [TG, NORM_RING, C])
        logit = sb("logit", [TG, G, E])
        best = sb("best", [TG, G, 8])
        best_at = sb("best_at", [TG, G, 8], U32)
        atf = sb("atf", [TG, G, 2])
        gap = sb("gap", [TG, G])
        egap = sb("egap", [TG, G])
        p1 = sb("p1", [TG, G])
        p2 = sb("p2", [TG, G])
        hot1 = sb("hot1", [TG, G, E])
        hot2 = sb("hot2", [TG, G, E])
        both = sb("both", [TG, G, E])
        cnt = sb("cnt", [TG, 2, G, E])
        cw = sb("cw", [TG, G, E])

        with ExitStack() as att_only:
            def sa(name, shape):
                return att_only.enter_context(nc.sbuf_tensor(name, shape, F32))
            qt = sa("qt", [128, 2, 6, TG])
            kt = sa("kt", [128, 2, 6, TG])
            v64 = sa("v64", [TG, 3, H, T5_D + 1])
            prob = sa("prob", [TG, 3, 3, TG])
            probt = sa("probt", [TG, 2, 3, TG])
            o = sa("o", [TG, 2, F])
            ot = sa("ot", [128, 6, TG])
        hid_hi = sb("hid_hi", [128, 2, FC, 3 * TP], F32R)
        hid_lo = sb("hid_lo", [128, 2, FC, 3 * TP], F32R)
        hid = sb("hid", [128, 2, 3 * TP])

        ps_turn = ps("ps_turn", [128, 512])
        ps_proj = ps("ps_proj", [128, 2, 512])
        ps_score = ps("ps_score", [128, 2, 512])
        ps_pt = ps("ps_pt", [128, 512])
        ps_o = ps("ps_o", [128, 2, 512])

        const_in = sem("const_in")
        patch_in = [sem(f"patch_in{i}") for i in range(PATCH_RING)]
        aw_in = [sem(f"aw_in{i}") for i in range(2)]
        fw_in = sem("fw_in")
        fw_hi = sem("fw_hi")
        fw_ready = sem("fw_ready")
        xhi_ready = sem("xhi_ready")
        hid_ready = sem("hid_ready")
        setup_done = sem("setup_done")
        aw_scaled = sem("aw_scaled")
        stats_ready = sem("stats_ready")
        norm_done = sem("norm_done")
        pool_step = sem("pool_step")
        turn_full = sem("turn_full")
        xt_ready = sem("xt_ready")
        proj_full = sem("proj_full")
        proj_taken = [sem(f"proj_taken{i}") for i in range(2)]
        score_full = sem("score_full")
        score_taken = [sem(f"score_taken{i}") for i in range(2)]
        shifted = sem("shifted")
        prob_ready = sem("prob_ready")
        pt_full = sem("pt_full")
        pt_taken = sem("pt_taken")
        o_full = sem("o_full")
        o_ready = sem("o_ready")
        gap_ready = sem("gap_ready")
        egap_ready = sem("egap_ready")
        hot_ready = sem("hot_ready")
        rows_done = sem("rows_done")
        out_done = sem("out_done")
        dve_step = sem("dve_step")

        ident = const[:, K_IDENT:K_IDENT + TG]
        band = const[:, K_BAND:K_BAND + TG]
        before_m = const[:, K_BEFORE:K_BEFORE + TG]
        ones_m = const[:, K_ONES:K_ONES + TG]
        iota = const[:, K_IOTA:K_IOTA + G * E].rearrange("p (g e) -> p g e", g=G)

        def aw_part(a, at, n):
            w = aw_small if a in (NEIGH, DIAG) else aw_big
            return w[:, at:at + 2 * n].rearrange("p (c n) -> p c n", c=2)

        aw_uses = {NEIGH: 16, DIAG: 32, CAUSAL: 16} | {T5 + l: 16 + 32 * (l + 1) for l in range(LAYERS)}

        def v_of(a):
            return v64 if ATTS[a].t5 else v16

        def unit(a, g, u):
            return (a * G + g) * 4 + u

        NCONST = 10

        def last_item(table, st):
            return max(n for key, n in table.items() if key[0] == st)

        block = ctx.enter_context(nc.Block())

        @block.sync
        def _(sp):
            for dst, src in ((const[:], consts), (tokw[:], tok_w), (row[:], rows), (gain[:], gains), (gainf[:], gains_ffn),
                             (gatew[:], gates_w), (hscale[:], head_scale), (relbias[:], bias_src),
                             (xband[KC:KC + 1, 0, 0, :], edge), (xband[KC:KC + 1, 1, 0, :], edge)):
                sp.dma_start(dst, src).then_inc(const_in, 16)

            def load_patch(g):
                if g >= PATCH_RING:
                    sp.wait_ge(proj_full, PROJ[(("att", 0), "TOK", g - PATCH_RING)] + 1)
                sp.dma_start(patch[:, g % PATCH_RING, :, :], patches[g]).then_inc(patch_in[g % PATCH_RING], 16)

            def load_aw(a):
                before = {DIAG: NEIGH, T5: CAUSAL}.get(a, a - 1)
                if a > CAUSAL:
                    sp.wait_ge(proj_full, last_item(PROJ, ("att", before)) + 1)
                    if a == DIAG:
                        sp.wait_ge(o_full, (NEIGH + 1) * G)
                src = (aw_neigh, aw_causal, aw_diag)[a] if a < T5 else aw_t5[a - T5]
                dst = aw_small if a in (NEIGH, DIAG) else aw_big
                sp.dma_start(dst[0:src.shape[0], 0:src.shape[1]], src).then_inc(aw_in[a % 2 if a < T5 else 1], 16)
                if a >= T5:
                    sp.dma_start(wo[:], wo_t5[a - T5]).then_inc(aw_in[1], 16)

            def load_fw(r):
                if r >= 1:
                    sp.wait_ge(fw_ready, r)
                sp.dma_start(w1_in[:].rearrange("p c n -> p (c n)"), w1_all[r]).then_inc(fw_in, 16)
                sp.dma_start(w2_in[:], w2_all[r]).then_inc(fw_in, 16)

            load_patch(0)
            load_patch(1)
            load_aw(0)
            load_aw(1)
            for g in range(PATCH_RING, G):
                load_patch(g)
            load_fw(0)
            for st in stages():
                for at, step in PROGRAM:
                    if at == st and step[0] == "W" and step[1] + 1 < NRUNS:
                        load_fw(step[1] + 1)
                if st[0] == "att":
                    a = st[1]
                    after = {NEIGH: DIAG, CAUSAL: T5, DIAG: None}.get(a, a + 1)
                    if after is not None and after < NATT:
                        load_aw(after)
            for g in range(G):
                n = min(TG, T_REAL - g * TG)
                sp.wait_ge(rows_done, g + 1)
                sp.dma_start(out[g * TG:g * TG + n, :], xn[0:n, g, 0:C]).then_inc(out_done, 16)
            sp.wait_ge(out_done, 16 * G)

        @block.tensor
        def _(pe):
            def proj_bank(key):
                n = PROJ[key]
                if n >= 2:
                    pe.wait_ge(proj_taken[n % 2], n // 2)
                return ps_proj[:, n % 2, :]

            def proj_out(key):
                n = PROJ[key]
                pe.wait_ge(proj_taken[n % 2], n // 2 + 1)

            def score_bank(key):
                n = SCORE[key]
                if n >= 2:
                    pe.wait_ge(score_taken[n % 2], n // 2)
                return ps_score[:, n % 2, :]

            def turn(st, g):
                n = TURNED[(st, "A", g)]
                pe.wait_ge(norm_done, READY[(st, g)] + 1)
                if n:
                    pe.wait_ge(xt_ready, n)
                src = x if st == ("att", DIAG) else xn
                if st[0] == "ffn":
                    for c in range(2):
                        last = pe.transpose(ps_turn[:, c * TP:c * TP + TG], src[:, g, c * 128:(c + 1) * 128], ident)
                    last.then_inc(turn_full, 1)
                    return
                for c in range(2):
                    last = pe.transpose(ps_turn[0:KC, c * TG:(c + 1) * TG], src[:, g, c * KC:(c + 1) * KC], ident)
                if st == ("att", NEIGH):
                    for c in range(2):
                        last = pe.matmul(ps_turn[0:KC, (2 + c) * TG:(3 + c) * TG], src[:, g, c * KC:(c + 1) * KC],
                                         band, start=True, stop=True)
                last.then_inc(turn_full, 1)

            def att_step(st, step):
                a = st[1]
                s = ATTS[a]
                kind, g = step[0], step[1]
                par = g % 2
                key = (st, *step)
                if kind == "A":
                    turn(st, g)
                elif kind == "TOK":
                    bank = proj_bank(key)
                    pe.wait_ge(patch_in[g % PATCH_RING], 16 * (g // PATCH_RING + 1))
                    for c in range(PCH):
                        last = pe.matmul(bank[0:TG, 0:C], patch[:, g % PATCH_RING, c, :], tokw[:, c, :],
                                         start=(c == 0), stop=(c == PCH - 1))
                    last.then_inc(proj_full, 1)
                elif kind in ("Q", "K"):
                    j = step[2]
                    bank = proj_bank(key)
                    if step == ("Q", 0, 0):
                        pe.wait_ge(aw_in[a % 2 if a < T5 else 1], aw_uses[a])
                        if a < T5:
                            pe.wait_ge(aw_scaled, a + 1)
                    pe.wait_ge(xt_ready, TURNED[(st, "A", g)] + 1)
                    width = F if s.t5 else QK_SMALL
                    which = 0 if kind == "Q" else 1
                    if a == NEIGH:
                        parts = [(aw_part(a, (2 * which + i) * 2 * width, width), i) for i in range(2)]
                    else:
                        parts = [(aw_part(a, which * 2 * width, width), 0)]
                    for i in range(3):
                        m = 3 * j + i
                        terms = []
                        for w, banded in parts:
                            for c in range(2):
                                k = KC + 1 if a == NEIGH and c == 0 else KC
                                src = xband[0:k, par, c, :] if banded else xt[0:k, par, c, :]
                                terms.append((w[0:k, c, m * 128:(m + 1) * 128], src))
                        for n, (w, src) in enumerate(terms):
                            last = pe.matmul(bank[:, i * TG:(i + 1) * TG], w, src, start=(n == 0),
                                             stop=(n == len(terms) - 1))
                    last.then_inc(proj_full, 1)
                elif kind == "V":
                    j = step[2]
                    bank = proj_bank(key)
                    width = F if s.t5 else C
                    at = (4 if s.t5 or a != NEIGH else 8) * (F if s.t5 else QK_SMALL)
                    w = aw_part(a, at, width)
                    n = width // s.items
                    for c in range(2):
                        k = KC + 1 if a == NEIGH and c == 0 else KC
                        last = pe.matmul(bank[0:TG, 0:n], xt[0:k, par, c, :], w[0:k, c, j * n:(j + 1) * n],
                                         start=(c == 0), stop=(c == 1))
                    last.then_inc(proj_full, 1)
                elif kind == "S":
                    u = step[2]
                    bank = score_bank(key)
                    if u == 0:
                        for what in ("Q", "K", "V"):
                            for j in range(s.items):
                                proj_out((st, what, g, j))
                    if s.pe_mask:
                        pe.matmul(bank[0:TG, 0:3 * TG], identb[:], maskb[:, a, :, :].rearrange("p h k -> p (h k)"),
                                  start=True, stop=False, skip_group_check=True)
                    for i, (c, p) in enumerate(s.heads(u)):
                        last = pe.matmul(bank[0:TG, i * TG:(i + 1) * TG], qt[p:p + s.rows, par, c, :],
                                         kt[p:p + s.rows, par, c, :], start=not s.pe_mask, stop=True,
                                         skip_group_check=True)
                    last.then_inc(score_full, 1)
                elif kind == "PT":
                    u = step[2]
                    n = unit(a, g, u)
                    pe.wait_ge(prob_ready, n + 1)
                    if n:
                        pe.wait_ge(pt_taken, n)
                    for i in range(3):
                        last = pe.transpose(ps_pt[0:TG, i * TG:(i + 1) * TG], prob[:, n % 3, i, :], ident)
                    last.then_inc(pt_full, 1)
                elif kind == "PV":
                    u = step[2]
                    pe.wait_ge(pt_taken, unit(a, g, u) + 1)
                    if u == 0 and a * G + g:
                        pe.wait_ge(o_ready, a * G + g)
                    v = v_of(a)
                    for i, (c, p) in enumerate(s.heads(u)):
                        h = s.head(c, p)
                        at = (h % 6) * (s.d + 1)
                        last = pe.matmul(ps_o[0:TG, h // 6, at:at + s.d + 1], probt[:, u % 2, i, :], v[:, (a * G + g) % 3, h, :],
                                         start=True, stop=True, skip_group_check=True)
                    if u == 3:
                        last.then_inc(o_full, 1)
                elif kind == "OT":
                    j = step[2]
                    bank = proj_bank(key)
                    pe.wait_ge(o_ready, a * G + g + 1)
                    n = s.ochunks // s.items
                    for i in range(n):
                        m = j * n + i
                        last = pe.transpose(bank[0:s.och, i * TG:(i + 1) * TG],
                                            o[:, par, m * s.och:(m + 1) * s.och], ident)
                    last.then_inc(proj_full, 1)
                elif kind == "Y":
                    bank = proj_bank(key)
                    for j in range(s.items):
                        proj_out((st, "OT", g, j))
                    if s.t5:
                        w = wo[:].rearrange("p (c n) -> p c n", c=FC)
                    else:
                        w = aw_part(a, 4 * QK_SMALL + 2 * C, C)
                    for c in range(s.ochunks):
                        last = pe.matmul(bank[0:TG, 0:C], ot[0:s.och, c, :], w[0:s.och, c, :],
                                         start=(c == 0), stop=(c == s.ochunks - 1))
                    last.then_inc(proj_full, 1)

            def ffn_step(st, step):
                f = st[1]
                kind = step[0]
                key = (st, *step)
                if kind == "A":
                    turn(st, step[1])
                elif kind == "L":
                    g = step[1]
                    bank = score_bank(key)
                    pe.wait_ge(xt_ready, TURNED[(st, "A", g)] + 1)
                    terms = [(xa_hi, gate_hi, 0), (xa_hi, gate_lo, 0), (xa_lo, gate_hi, 0), (xb, gate_hi, 1),
                             (xb, gate_lo, 1)]
                    for i, (src, w, c) in enumerate(terms):
                        last = pe.matmul(bank[0:TG, 0:E], src[:, g, 0:TG], w[:, c, WG[f], :], start=(i == 0),
                                         stop=(i == len(terms) - 1))
                    last.then_inc(score_full, 1)
                elif kind == "CNT":
                    bank = score_bank(key)
                    pe.wait_ge(hot_ready, 1)
                    rhs = both[:].rearrange("p g e -> p (g e)")
                    pe.matmul(bank[0:TG, 0:G * E], before_m, rhs, start=True, stop=True)
                    pe.matmul(bank[0:TG, G * E:2 * G * E], ones_m, rhs, start=True, stop=True).then_inc(score_full, 1)
                elif kind == "U":
                    _, k, b, m = step
                    r = RUN0[f] + k
                    slot = r % FW_RING
                    bank = proj_bank(key)
                    if m == 0 and b == 0:
                        pe.wait_ge(fw_ready, r + 1)
                    g0, n = BLOCKS[b]
                    if m == 0 and k == 0:
                        pe.wait_ge(xt_ready, TURNED[(st, "A", g0 + n - 1)] + 1)
                    terms = [(w1_hi, 0, xa_hi), (w1_hi, 0, xa_lo), (w1_lo, 0, xa_hi), (w1_hi, 1, xb), (w1_lo, 1, xb)]
                    for i, (w, c, src) in enumerate(terms):
                        last = pe.matmul(bank[:, 0:n * TP], w[:, slot, c, m * 128:(m + 1) * 128],
                                         src[:, g0:g0 + n, :].rearrange("p g t -> p (g t)"), start=(i == 0),
                                         stop=(i == len(terms) - 1))
                    last.then_inc(proj_full, 1)
                elif kind == "D":
                    _, k, g = step
                    r = RUN0[f] + k
                    slot = r % FW_RING
                    bank = score_bank(key)
                    b = BLOCK_OF[g]
                    if g == BLOCKS[b][0]:
                        pe.wait_ge(hid_ready, HIDDEN[(st, "U", k, b, FC - 1)] + 1)
                    at = (g - BLOCKS[b][0]) * TP
                    for m in range(FC):
                        for i, (src, w) in enumerate(((hid_hi, w2_hi), (hid_hi, w2_lo), (hid_lo, w2_hi))):
                            last = pe.matmul(bank[0:TG, 0:C], src[:, b % 2, m, at:at + TG], w[:, slot, m, :],
                                             start=(m == 0 and i == 0), stop=(m == FC - 1 and i == 2))
                    last.then_inc(score_full, 1)

            pe.wait_ge(const_in, 16 * NCONST)
            pe.wait_ge(setup_done, 1)
            for st, step in PROGRAM:
                (att_step if st[0] == "att" else ffn_step)(st, step)

        @block.scalar
        def _(act):
            def take_proj(key):
                n = PROJ[key]
                act.wait_ge(proj_full, n + 1)
                return ps_proj[:, n % 2, :], proj_taken[n % 2]

            def turned(st, g):
                n = TURNED[(st, "A", g)]
                act.wait_ge(turn_full, n + 1)
                if st[0] == "ffn":
                    f = st[1]
                    act.activation(xa_hi[:, g, 0:TG], ps_turn[:, 0:TG], ACT.Copy, scale=gainf[:, 0, f:f + 1])
                    act.activation(xb[:, g, 0:TG], ps_turn[:, TP:TP + TG], ACT.Copy,
                                   scale=gainf[:, 1, f:f + 1]).then_inc(xhi_ready, 1)
                    return
                if st in GAIN:
                    for c in range(2):
                        last = act.activation(xt[0:KC, g % 2, c, :], ps_turn[0:KC, c * TG:(c + 1) * TG], ACT.Copy,
                                              scale=gain[:, c, GAIN[st]:GAIN[st] + 1])
                else:
                    last = act.activation(xt[0:KC, g % 2, :, :],
                                          ps_turn[0:KC, 0:2 * TG].rearrange("p (c n) -> p c n", c=2), ACT.Copy)
                    if st == ("att", NEIGH):
                        last = act.activation(xband[0:KC, g % 2, :, :],
                                              ps_turn[0:KC, 2 * TG:4 * TG].rearrange("p (c n) -> p c n", c=2), ACT.Copy)
                last.then_inc(xt_ready, 1)

            act.wait_ge(const_in, 16 * NCONST)
            act.wait_ge(setup_done, 1)
            gates = 0
            for st, step in PROGRAM:
                kind = step[0]
                key = (st, *step)
                if kind == "A":
                    turned(st, step[1])
                elif kind in ("Q", "K"):
                    bank, taken = take_proj(key)
                    j = step[2]
                    dst = qt if kind == "Q" else kt
                    act.activation(dst[:, step[1] % 2, 3 * j:3 * j + 3, :],
                                   bank[:, 0:3 * TG].rearrange("p (c n) -> p c n", c=3), ACT.Copy).then_inc(taken, 1)
                elif kind == "E":
                    _, g, u = step
                    a = st[1]
                    n = SCORE[(st, "S", g, u)]
                    if ATTS[a].t5:
                        act.wait_ge(shifted, unit(a - T5, g, u) + 1)
                    else:
                        act.wait_ge(score_taken[n % 2], n // 2 + 1)
                    act.activation(prob[:, unit(a, g, u) % 3, :, :], prob[:, unit(a, g, u) % 3, :, :], ACT.Exp).then_inc(prob_ready, 1)
                elif kind == "PT":
                    _, g, u = step
                    act.wait_ge(pt_full, unit(st[1], g, u) + 1)
                    act.activation(probt[:, u % 2, :, :], ps_pt[0:TG, 0:3 * TG].rearrange("p (c n) -> p c n", c=3),
                                   ACT.Copy).then_inc(pt_taken, 1)
                elif kind == "OT":
                    bank, taken = take_proj(key)
                    _, g, j = step
                    s = ATTS[st[1]]
                    n = s.ochunks // s.items
                    act.activation(ot[0:s.och, j * n:(j + 1) * n, :],
                                   bank[0:s.och, 0:n * TG].rearrange("p (c n) -> p c n", c=n),
                                   ACT.Copy).then_inc(taken, 1)
                elif kind == "GATE":
                    gates += 1
                    act.wait_ge(gap_ready, gates)
                    act.activation(egap[:], gap[:], ACT.Exp).then_inc(egap_ready, 1)
                elif kind == "U":
                    bank, taken = take_proj(key)
                    _, k, b, m = step
                    n = BLOCKS[b][1] * TP
                    h = HIDDEN[key]
                    func = ACT.Relu if ffn_runs(st[1])[k] < 0 else ACT.Gelu
                    if h >= 2:
                        act.wait_ge(hid_ready, h - 1)
                    act.activation(hid[:, h % 2, 0:n], bank[:, 0:n], func)
                    act.activation(hid_hi[:, b % 2, m, 0:n], bank[:, 0:n], func).then_inc(taken, 1)
                elif kind == "W":
                    r = step[1]
                    act.wait_ge(fw_in, 32 * (r + 1))
                    act.activation(w1_hi[:, r % FW_RING, :, :], w1_in[:], ACT.Copy)
                    act.activation(w2_hi[:, r % FW_RING, :, :].rearrange("p m c -> p (m c)"), w2_in[:],
                                   ACT.Copy).then_inc(fw_hi, 1)

        @block.gpsimd
        def _(pool):
            steps = [0]

            def link(ins):
                steps[0] += 1
                ins.then_inc(pool_step, 1)
                pool.wait_ge(pool_step, steps[0])

            pool.wait_ge(const_in, 16 * NCONST)
            pool.wait_ge(setup_done, 1)
            for (st, kind, g), n in NORMS.items():
                m = n % NORM_RING
                v, r, t = var[:, m:m + 1], rs[:, m:m + 1], tmp[:, 0:1]
                pool.wait_ge(stats_ready, n + 1)
                for _ in range(3):
                    link(pool.tensor_tensor(t, r, r, ALU.mult))
                    link(pool.tensor_tensor(t, t, v, ALU.mult))
                    link(pool.tensor_scalar(t, t, -0.5, 1.5, ALU.mult, ALU.add))
                    link(pool.tensor_tensor(r, r, t, ALU.mult))
                mean, xg, xng = mv[:, m, 0:1], x[:, g, :], xn[:, g, 0:C]

                def centred(dst, src):
                    return pool.tensor_scalar(dst, src, mean, r, ALU.subtract, ALU.mult)

                def scaled(dst, src):
                    return pool.tensor_scalar(dst, src, r, None, ALU.mult)

                if kind == "TOK":
                    link(centred(xng, xg))
                    link(pool.tensor_tensor(xng, xng, row[:, R_LNG, :], ALU.mult))
                    last = pool.tensor_tensor(xng, xng, row[:, R_LNB, :], ALU.add)
                elif kind == "N2":
                    last = (centred if st == ("att", NEIGH) else scaled)(xng, xg)
                elif st in (("att", NEIGH), ("att", DIAG)):
                    link(centred(xg, wide[:, m, :]))
                    last = pool.tensor_copy(held[:, g, :], xg)
                elif st == ("ffn", 0):
                    last = centred(xg, wide[:, m, :])
                elif st == ("att", CAUSAL):
                    last = centred(xng, xg)
                elif st == ("ffn", LAYERS):
                    link(scaled(xng, xg))
                    link(pool.tensor_tensor(xng, xng, row[:, R_LNF, :], ALU.mult))
                    last = pool.tensor_tensor(held[:, g, :], held[:, g, :], xng, ALU.add)
                else:
                    last = scaled(xng, xg)
                if kind == "Y" and st != ("att", DIAG):
                    link(last)
                    last = pool.tensor_copy(xn[:, g, C:CX], xn[:, g, 128:C])
                last.then_inc(norm_done, 1)

        @block.vector
        def _(dve):
            steps = [0]

            def link(ins):
                steps[0] += 1
                ins.then_inc(dve_step, 1)
                dve.wait_ge(dve_step, steps[0])

            def tell(ins, which, value):
                ins.then_inc(which, 1)
                dve.wait_ge(which, value)

            def start_norm(key, src, rms, eps):
                n = NORMS[key]
                m = n % NORM_RING
                link(dve.bn_stats(stat[:], src))
                link(dve.bn_aggr(mv[:, m, :], stat[:]))
                v, r = var[:, m:m + 1], rs[:, m:m + 1]
                if rms:
                    link(dve.scalar_tensor_tensor(out=mv[:, m, 1:2], in0=mv[:, m, 0:1], scalar=mv[:, m, 0:1],
                                                  in1=mv[:, m, 1:2], op0=ALU.mult, op1=ALU.add))
                link(dve.tensor_scalar(v, mv[:, m, 1:2], eps, None, ALU.add))
                tell(dve.tensor_scalar(r.bitcast(I32), v.bitcast(I32), -0.5, RSQRT_SEED, ALU.mult, ALU.add),
                     stats_ready, n + 1)

            def norm_slot(key):
                n = NORMS[key]
                if n >= NORM_RING:
                    dve.wait_ge(norm_done, n - NORM_RING + 1)
                return n % NORM_RING

            def take_proj(key):
                n = PROJ[key]
                dve.wait_ge(proj_full, n + 1)
                return ps_proj[:, n % 2, :], proj_taken[n % 2], n // 2 + 1

            def take_score(key):
                n = SCORE[key]
                dve.wait_ge(score_full, n + 1)
                return ps_score[:, n % 2, :], score_taken[n % 2], n // 2 + 1

            def softmax_shift(st, step):
                a, (_, g, u) = st[1], step
                bank, taken, value = take_score((st, *step))
                scores = bank[0:TG, 0:3 * TG].rearrange("p (h k) -> p h k", h=3)
                dst = prob[:, unit(a, g, u) % 3, :, :]
                if ATTS[a].t5:
                    tell(dve.tensor_tensor(dst, scores, relbias[:, 3 * u:3 * u + 3, :], ALU.add), taken, value)
                    scores = dst
                link(dve.tensor_reduce(negmax[:], scores, AX.X, ALU.max, negate=True))
                ins = dve.tensor_tensor(dst, scores, negmax[:].unsqueeze(2).to_broadcast([TG, 3, TG]), ALU.add)
                if ATTS[a].t5:
                    tell(ins, shifted, unit(a - T5, g, u) + 1)
                else:
                    tell(ins, taken, value)

            def divide(a, g):
                s = ATTS[a]
                dve.wait_ge(o_full, a * G + g + 1)
                n = 6 * (s.d + 1)
                view = ps_o[0:TG, :, 0:n].rearrange("p b (h d) -> p b h d", h=6)
                link(dve.reciprocal(rden[:].rearrange("p (b h) -> p b h", b=2), view[:, :, :, s.d]))
                for b in range(2):
                    ins = dve.tensor_tensor(
                        o[:, g % 2, b * 6 * s.d:(b + 1) * 6 * s.d].rearrange("p (h d) -> p h d", h=6),
                        view[:, b, :, 0:s.d],
                        rden[:, 6 * b:6 * b + 6].unsqueeze(2).to_broadcast([TG, 6, s.d]), ALU.mult)
                    if b == 0:
                        link(ins)
                tell(ins, o_ready, a * G + g + 1)

            dve.wait_ge(const_in, 16 * NCONST)
            link(dve.tensor_copy(identb[:], ident))
            for a, at in enumerate((K_BLOCK, K_CAUSAL, K_DIAG)):
                for i in range(3):
                    link(dve.tensor_copy(maskb[:, a, i, :], const[:, at:at + TG]))
            link(dve.tensor_tensor(relbias[:], relbias[:],
                                   const[:, K_BLOCK:K_BLOCK + TG].unsqueeze(1).to_broadcast([TG, H, TG]), ALU.add))
            link(dve.memset(v16[:], 1.0))
            link(dve.memset(xt[KC:KC + 1, :, 0, :], 1.0))
            for t in (xa_hi, xa_lo, xb):
                link(dve.memset(t[:, :, TG:TP].bitcast(F32), 0.0))
            link(dve.memset(w1_lo[64:128, :, 1, :].bitcast(F32), 0.0))
            link(dve.memset(gate_lo[64:128, 1, :, :].bitcast(F32), 0.0))
            link(dve.tensor_copy(gate_hi[:], gatew[:]))
            link(dve.tensor_tensor(gate_lo[:, 0, :, :], gatew[:, 0, :, :], gate_hi[:, 0, :, :].bitcast(F32),
                                   ALU.subtract))
            link(dve.tensor_tensor(gate_lo[0:64, 1, :, :], gatew[0:64, 1, :, :], gate_hi[0:64, 1, :, :].bitcast(F32),
                                   ALU.subtract))
            link(dve.tensor_tensor(row[:, R_POS, :], row[:, R_POS, :], row[:, R_TOKB, :], ALU.add))
            tell(dve.memset(rden[:], 0.0), setup_done, 1)

            def scale_weights(a):
                dve.wait_ge(aw_in[a % 2], aw_uses[a])
                n = 2 * QK_SMALL
                if a == NEIGH:
                    s = float(SMALL_D) ** -0.5
                    link(dve.tensor_scalar(aw_small[:, 0:n], aw_small[:, 0:n], 1.2 * s, None, ALU.mult))
                    ins = dve.tensor_scalar(aw_small[:, n:2 * n], aw_small[:, n:2 * n], -0.2 * s, None, ALU.mult)
                elif a == CAUSAL:
                    ins = dve.tensor_scalar(aw_big[:, 0:n], aw_big[:, 0:n], float(SMALL_D) ** -0.5, None, ALU.mult)
                else:
                    w = aw_part(DIAG, 0, QK_SMALL)[0:KC]
                    ins = dve.tensor_tensor(w, w, hscale[:].unsqueeze(1).to_broadcast([KC, 2, QK_SMALL]), ALU.mult)
                tell(ins, aw_scaled, a + 1)

            gates = 0
            for st, step in PROGRAM:
                kind = step[0]
                key = (st, *step)
                if kind == "SC":
                    scale_weights(step[1])
                elif kind == "TOK":
                    g = step[1]
                    bank, taken, value = take_proj(key)
                    tell(dve.tensor_tensor(x[:, g, :], bank[0:TG, 0:C], row[:, R_POS, :], ALU.add), taken, value)
                    norm_slot((st, "TOK", g))
                    start_norm((st, "TOK", g), x[:, g, :], False, LN_EPS)
                elif kind == "A" and st[0] == "ffn":
                    g, f = step[1], st[1]
                    n = TURNED[key]
                    dve.wait_ge(xhi_ready, sum(1 for k, v in TURNED.items() if k[0][0] == "ffn" and v <= n))
                    link(dve.scalar_tensor_tensor(
                        out=xa_lo[:, g, 0:TG], in0=ps_turn[:, 0:TG], scalar=gainf[:, 0, f:f + 1],
                        in1=xa_hi[:, g, 0:TG].bitcast(F32), op0=ALU.mult, op1=ALU.subtract))
                    tell(dve.scalar_tensor_tensor(
                        out=xb[64:128, g, 0:TG], in0=ps_turn[64:128, TP:TP + TG], scalar=gainf[64:128, 1, f:f + 1],
                        in1=xb[64:128, g, 0:TG].bitcast(F32), op0=ALU.mult, op1=ALU.subtract), xt_ready, n + 1)
                elif kind == "W":
                    r = step[1]
                    dve.wait_ge(fw_hi, r + 1)
                    slot = r % FW_RING
                    link(dve.tensor_tensor(w1_lo[:, slot, 0, :], w1_in[:, 0, :],
                                           w1_hi[:, slot, 0, :].bitcast(F32), ALU.subtract))
                    link(dve.tensor_tensor(w1_lo[0:64, slot, 1, :], w1_in[0:64, 1, :],
                                           w1_hi[0:64, slot, 1, :].bitcast(F32), ALU.subtract))
                    tell(dve.tensor_tensor(w2_lo[:, slot, :, :].rearrange("p m c -> p (m c)"), w2_in[:],
                                           w2_hi[:, slot, :, :].rearrange("p m c -> p (m c)").bitcast(F32),
                                           ALU.subtract), fw_ready, r + 1)
                elif kind == "U":
                    _, k, b, m = step
                    n, h = BLOCKS[b][1] * TP, HIDDEN[key]
                    dve.wait_ge(proj_taken[PROJ[key] % 2], PROJ[key] // 2 + 1)
                    tell(dve.tensor_tensor(hid_lo[:, b % 2, m, 0:n], hid[:, h % 2, 0:n],
                                           hid_hi[:, b % 2, m, 0:n].bitcast(F32), ALU.subtract), hid_ready, h + 1)
                elif kind == "V":
                    _, g, j = step
                    bank, taken, value = take_proj(key)
                    s = ATTS[st[1]]
                    hs = H // s.items
                    if s.t5:
                        link(dve.memset(v64[:, (st[1] * G + g) % 3, j * hs:(j + 1) * hs, s.d:s.d + 1], 1.0))
                    tell(dve.tensor_copy(v_of(st[1])[:, (st[1] * G + g) % 3, j * hs:(j + 1) * hs, 0:s.d],
                                         bank[0:TG, 0:hs * s.d].rearrange("p (h d) -> p h d", h=hs)), taken, value)
                elif kind == "S":
                    softmax_shift(st, step)
                elif kind == "PV" and step[2] == 3:
                    g = step[1]
                    divide(st[1], g)
                    if st[1] == NEIGH:
                        m = norm_slot((st, "PV", g))
                        link(dve.tensor_tensor(wide[:, m, :], o[:, g % 2, 0:C], x[:, g, :], ALU.add))
                        start_norm((st, "PV", g), wide[:, m, :], False, LN_EPS)
                elif kind == "Y":
                    g, a = step[1], st[1]
                    bank, taken, value = take_proj(key)
                    y = bank[0:TG, 0:C]
                    m = norm_slot((st, "Y", g))
                    if a == DIAG:
                        tell(dve.scalar_tensor_tensor(out=wide[:, m, :], in0=x[:, g, :], scalar=2.0, in1=y,
                                                      op0=ALU.mult, op1=ALU.add), taken, value)
                        link(dve.tensor_tensor(wide[:, m, :], wide[:, m, :], row[:, R_BPROJ, :], ALU.add))
                        start_norm((st, "Y", g), wide[:, m, :], False, LN_EPS)
                    else:
                        tell(dve.tensor_tensor(x[:, g, :], y, x[:, g, :], ALU.add), taken, value)
                        start_norm((st, "Y", g), x[:, g, :], a >= T5, RMS_EPS if a >= T5 else LN_EPS)
                elif kind == "N2":
                    g = step[1]
                    before = "PV" if st == ("att", NEIGH) else "Y"
                    dve.wait_ge(norm_done, NORMS[(st, before, g)] + 1)
                    norm_slot((st, "N2", g))
                    rms = st == ("att", DIAG)
                    start_norm((st, "N2", g), x[:, g, :], rms, RMS_EPS if rms else LN_EPS)
                elif kind == "FIN":
                    g = step[1]
                    dve.wait_ge(norm_done, NORMS[(st, "D", g)] + 1)
                    link(dve.bn_stats(stat[:], held[:, g, :]))
                    link(dve.bn_aggr(last_mv[:], stat[:]))
                    v, r, t = last_nr[:, 0:1], last_nr[:, 1:2], last_nr[:, 2:3]
                    link(dve.tensor_scalar(v, last_mv[:, 1:2], LN_EPS, None, ALU.add))
                    link(dve.tensor_scalar(r.bitcast(I32), v.bitcast(I32), -0.5, RSQRT_SEED, ALU.mult, ALU.add))
                    for _ in range(3):
                        link(dve.tensor_tensor(t, r, r, ALU.mult))
                        link(dve.tensor_tensor(t, t, v, ALU.mult))
                        link(dve.tensor_scalar(t, t, -0.5, 1.5, ALU.mult, ALU.add))
                        link(dve.tensor_tensor(r, r, t, ALU.mult))
                    tell(dve.tensor_scalar(xn[:, g, 0:C], held[:, g, :], last_mv[:, 0:1], r, ALU.subtract,
                                           ALU.mult), rows_done, g + 1)
                elif kind == "L":
                    g = step[1]
                    bank, taken, value = take_score(key)
                    tell(dve.tensor_copy(logit[:, g, :], bank[0:TG, 0:E]), taken, value)
                    link(dve.max(best[:, g, :], logit[:, g, :]))
                    link(dve.max_index(best_at[:, g, :], best[:, g, :], logit[:, g, :]))
                    if g == G - 1:
                        link(dve.tensor_copy(atf[:], best_at[:, :, 0:2]))
                        for k, hot in enumerate((hot1, hot2)):
                            link(dve.tensor_tensor(hot[:], iota, atf[:, :, k:k + 1].to_broadcast([TG, G, E]),
                                                   ALU.is_equal))
                        if st[1] == 0:
                            tell(dve.tensor_tensor(both[:], hot1[:], hot2[:], ALU.add), hot_ready, 1)
                elif kind == "CNT":
                    bank, taken, value = take_score(key)
                    tell(dve.tensor_copy(cnt[:].rearrange("p a g e -> p (a g e)"), bank[0:TG, 0:2 * G * E]),
                         taken, value)
                    for g in range(1, G - 1):
                        link(dve.tensor_tensor(cnt[:, 1, g, :], cnt[:, 1, g, :], cnt[:, 1, g - 1, :], ALU.add))
                    link(dve.tensor_tensor(cnt[:, 0, 1:G, :], cnt[:, 0, 1:G, :], cnt[:, 1, 0:G - 1, :], ALU.add))
                elif kind == "GATE":
                    gates += 1
                    tell(dve.tensor_tensor(gap[:], best[:, :, 1], best[:, :, 0], ALU.subtract), gap_ready, gates)
                    dve.wait_ge(egap_ready, gates)
                    link(dve.tensor_scalar(p1[:], egap[:], 1.0, None, ALU.add))
                    link(dve.reciprocal(p1[:], p1[:]))
                    link(dve.tensor_tensor(p2[:], p1[:], egap[:], ALU.mult))
                    link(dve.tensor_tensor(hot1[:], hot1[:], p1[:].unsqueeze(2).to_broadcast([TG, G, E]), ALU.mult))
                    link(dve.tensor_tensor(hot2[:], hot2[:], p2[:].unsqueeze(2).to_broadcast([TG, G, E]), ALU.mult))
                    link(dve.tensor_tensor(cw[:], hot1[:], hot2[:], ALU.add))
                    if st[1] == 0:
                        link(dve.scalar_tensor_tensor(
                            out=cw[:].rearrange("p g e -> p (g e)"),
                            in0=cnt[:, 0, :, :].rearrange("p g e -> p (g e)"), scalar=float(CAP),
                            in1=cw[:].rearrange("p g e -> p (g e)"), op0=ALU.is_lt, op1=ALU.mult))
                elif kind == "D":
                    _, k, g = step
                    f = st[1]
                    runs = ffn_runs(f)
                    bank, taken, value = take_score(key)
                    e = runs[k]
                    if e < 0:
                        ins = dve.tensor_tensor(x[:, g, :], bank[0:TG, 0:C], x[:, g, :], ALU.add)
                    else:
                        ins = dve.scalar_tensor_tensor(out=x[:, g, :], in0=bank[0:TG, 0:C],
                                                       scalar=cw[:, g, e:e + 1], in1=x[:, g, :], op0=ALU.mult,
                                                       op1=ALU.add)
                    tell(ins, taken, value)
                    if k == len(runs) - 1:
                        m = norm_slot((st, "D", g))
                        if f == 0:
                            link(dve.tensor_tensor(wide[:, m, :], held[:, g, :], x[:, g, :], ALU.add))
                            start_norm((st, "D", g), wide[:, m, :], False, LN_EPS)
                        else:
                            start_norm((st, "D", g), x[:, g, :], True, RMS_EPS)


def lay_out(inp):
    f = {k: np.asarray(v) for k, v in inp.items()}
    x = f["x"]
    z = np.zeros((G * IPG, NTOK, PD), np.float32)
    p = x.reshape(B, CIN, GRID, PATCH, GRID, PATCH).transpose(0, 2, 4, 1, 3, 5).reshape(B, GRID * GRID, PD)
    z[:B, 1:] = p
    patches = z.reshape(G, TG, PCH, 128).transpose(0, 3, 2, 1)

    def chunks(w, k):
        return w.reshape(-1, k, w.shape[-1]).transpose(1, 0, 2)

    def flat(w):
        return w.reshape(w.shape[0], -1)

    t = np.arange(TG)
    same = (t[:, None] // NTOK) == (t[None, :] // NTOK)
    const = np.zeros((TG, K_WIDTH), np.float32)
    const[:, K_IDENT:K_IDENT + TG] = np.eye(TG)
    const[:, K_BAND:K_BAND + TG] = same & (abs(t[:, None] - t[None, :]) <= 1)
    const[:, K_BLOCK:K_BLOCK + TG] = np.where(same, 0.0, NEG)
    const[:, K_CAUSAL:K_CAUSAL + TG] = np.where(same & (t[:, None] >= t[None, :]), 0.0, NEG)
    const[:, K_DIAG:K_DIAG + TG] = np.where(same & (t[:, None] != t[None, :]), 0.0, NEG)
    const[:, K_BEFORE:K_BEFORE + TG] = t[:, None] < t[None, :]
    const[:, K_ONES:K_ONES + TG] = 1.0
    const[:, K_IOTA:] = np.tile(np.arange(E), G)
    edge = np.where((t % NTOK == 0) | (t % NTOK == NTOK - 1), 2.0, 3.0).astype(np.float32)[None]

    rows = np.zeros((TG, 6, C), np.float32)
    rows[:, R_LNG] = f["L0_attn_ln_g"]
    rows[:, R_LNB] = f["L0_attn_ln_b"]
    rows[:, R_BPROJ] = f["L1_attn_b_proj"]
    rows[:, R_LNF] = f["L1_ffn_ln_f"]
    pos = f["L0_tok_positions"]
    ih = np.arange(GRID) * pos.shape[2] // GRID
    pos = pos[0][:, ih][:, :, ih].reshape(C, GRID * GRID).T
    for i in range(IPG):
        rows[i * NTOK, R_POS] = f["L0_tok_cls_embedding"][0, 0]
        rows[i * NTOK + 1:(i + 1) * NTOK, R_POS] = pos
        rows[i * NTOK + 1:(i + 1) * NTOK, R_TOKB] = f["L0_tok_b"]

    gains = np.zeros((NGAIN, C), np.float32)
    gains[0], gains[1] = f["L0_ffn_ln1_w"], f["L0_ffn_ln2_w"]
    gains[2::2], gains[3::2] = f["L1_ffn_ln1"], f["L1_ffn_ln2"]
    gains = gains.reshape(NGAIN, 2, KC).transpose(2, 1, 0)

    def twice(w):
        return np.stack([w[:128], np.concatenate([w[128:], w[128:]])], 1)

    gains_ffn = twice(np.stack([f["L0_ffn_ln2_w"]] + list(f["L1_ffn_ln2"]), 1))
    gw = np.stack([f["L0_ffn_w_g"].T, f["L1_ffn_gate_w"][0], f["L1_ffn_gate_w"][1]], 1)
    gw = twice(gw.reshape(C, 3 * E)).reshape(128, 2, 3, E)
    hs = np.broadcast_to(np.repeat(f["L1_attn_scale"], 32)[None], (KC, QK_SMALL))

    rel = np.arange(NTOK)[None, :] - np.arange(NTOK)[:, None]
    nb, maxd = f["L1_ffn_rel_emb"].shape[0] // 2, 128
    n = np.abs(rel)
    me = nb // 2
    nf = np.maximum(n, 1).astype(np.float32)
    large = me + (np.log(nf / np.float32(me)) / np.float32(np.log(maxd / me)) * np.float32(nb - me)).astype(np.int32)
    buckets = (rel > 0) * nb + np.where(n < me, n, np.minimum(large, nb - 1))
    heads = [ATTS[T5].head(c, s) for u in range(4) for c, s in ATTS[T5].heads(u)]
    bias = np.zeros((TG, H, TG), np.float32)
    for i in range(IPG):
        sl = slice(i * NTOK, (i + 1) * NTOK)
        bias[sl, :, sl] = f["L1_ffn_rel_emb"][buckets].transpose(0, 2, 1)[:, heads]

    def spread(w, at):
        out = np.zeros((w.shape[0], H, 32), np.float32)
        out[:, :, at:at + SMALL_D] = w.reshape(-1, H, SMALL_D)
        return out.reshape(-1, QK_SMALL)

    def with_bias(w, b):
        out = np.zeros((KC + 1, 2, w.shape[1]), np.float32)
        out[:KC] = chunks(w, KC)
        out[KC, 0] = b
        return flat(out)

    w, b = f["L0_attn_qkv_w"].T, f["L0_attn_qkv_b"][None]
    aw_neigh = np.concatenate(
        [with_bias(spread(w[:, i * C:(i + 1) * C], at), spread(b[:, i * C:(i + 1) * C], at)[0])
         for i in range(2) for at in (0, SMALL_D)] + [with_bias(w[:, 2 * C:], b[0, 2 * C:])], 1)

    def small(w, wo):
        w = w.T
        return np.concatenate([flat(chunks(spread(w[:, i * C:(i + 1) * C], 0), KC)) for i in range(2)]
                              + [flat(chunks(w[:, 2 * C:], KC)), flat(chunks(wo.T, KC))], 1)

    aw_causal = small(f["L0_ffn_c_attn_w"], f["L0_ffn_c_proj_w"])
    aw_diag = small(f["L1_attn_w_qkv"], f["L1_attn_w_proj"])
    aw_t5 = np.stack([np.concatenate([flat(chunks(f[f"L1_ffn_attn_{n}"][l], KC)) for n in "qkv"], 1)
                      for l in range(LAYERS)])
    wo_t5 = np.stack([flat(chunks(f["L1_ffn_attn_o"][l], 128)) for l in range(LAYERS)])
    up, down = list(f["L0_ffn_c_fc"]), list(f["L0_ffn_c_proj_e"])
    for l in range(LAYERS):
        up.append(f["L1_ffn_ffn_wi"][l])
        down.append(f["L1_ffn_ffn_wo"][l])
        if l in MOE_LAYERS:
            up += list(f["L1_ffn_moe_w1"][MOE_LAYERS.index(l)])
            down += list(f["L1_ffn_moe_w2"][MOE_LAYERS.index(l)])
    w1 = np.stack([flat(twice(w)) for w in up])
    w2 = np.stack([flat(chunks(w, 128)) for w in down])
    out = [patches, chunks(f["L0_tok_W"], 128), const, rows, gains, gains_ffn, gw, hs, bias, edge,
           aw_neigh, aw_causal, aw_diag, aw_t5, wo_t5, w1, w2]
    return [np.ascontiguousarray(a, dtype=np.float32) for a in out]


def kernel(**inputs):
    import concourse.bacc as bacc
    from concourse.bass_utils import run_bass_kernel_spmd

    nc = bacc.Bacc("TRN2", target_bir_lowering=False, num_devices=1)
    names = ["patches", "tok_w", "consts", "rows", "gains", "gains_ffn", "gates_w", "head_scale", "bias_src", "edge", "aw_neigh",
             "aw_causal", "aw_diag", "aw_t5", "wo_t5", "w1_all", "w2_all"]
    arrays = {n + "_dram": a for n, a in zip(names, lay_out(inputs))}
    args = [nc.dram_tensor(n, a.shape, F32, kind="ExternalInput").ap() for n, a in arrays.items()]
    out = nc.dram_tensor("out_dram", (T_REAL, C), F32, kind="ExternalOutput").ap()
    tower(nc, *args, out)
    r = run_bass_kernel_spmd(nc, [arrays], core_ids=[0])
    return r.results[0]["out_dram"].reshape(B, NTOK, C)
```
